# Optimizing a Trainium2 kernel written in Bass

```python
import numpy as np
import jax
import jax.numpy as jnp

def _softmax(x, axis=-1):
    return jax.nn.softmax(x, axis=axis)

def _gelu(x):
    return jax.nn.gelu(x, approximate=True)

def _silu(x):
    return jax.nn.silu(x)

def _sigmoid(x):
    return jax.nn.sigmoid(x)

def _layernorm(x, axis=-1, eps=1e-05):
    m = jnp.mean(x, axis=axis, keepdims=True)
    v = jnp.var(x, axis=axis, keepdims=True)
    return (x - m) / jnp.sqrt(v + eps)

def _scatter_add(tgt, idx, src, axis=0):
    return tgt.at[idx].add(src)

def _segment_sum(src, seg, n):
    return jax.ops.segment_sum(src, seg, n)
kernel_name = 'mk_adj_preln_d2_adj_r2_fe60d5'

def setup_inputs(seed: int=0):
    np.random.seed(seed)
    _w = jnp.asarray

    def _rec_inputs():
        import jax
        import jax.numpy as jnp
        _gk = jax.random.key(seed)
        x = -0.0005207 + 1.001 * jax.random.normal(jax.random.fold_in(_gk, 1), (64, 128, 128), jnp.float32)
        _w = (1.0 + jnp.arange(128, dtype=jnp.float32)) ** (-0.5)
        _w = _w / _w.mean()
        _pij = jnp.clip(0.03125 * _w[:, None] * _w[None, :], 0.0, 1.0)
        _a = jax.random.uniform(jax.random.fold_in(_gk, 2), (128, 128)) < _pij
        _a = jnp.logical_or(_a, jnp.eye(128, dtype=bool))
        _af = _a.astype(jnp.float32)
        adj = _af
        return (x, adj)
    x, adj = _rec_inputs()

    def _L0_gnn_setup():
        import jax, jax.numpy as jnp
        import numpy as np
        B, N, IN_DIM, OUT_DIM, H = (2, 2048, 128, 128, 4)
        HEAD_DIM = OUT_DIM // H
        EDGE_P = 0.01
        key = jax.random.key(seed)
        k1, k2, k3 = jax.random.split(key, 3)
        h = jax.random.normal(k1, (B, N, IN_DIM), dtype=jnp.float32)
        W = jax.random.normal(k2, (IN_DIM, 3 * OUT_DIM), dtype=jnp.float32) / np.sqrt(IN_DIM)
        adj = (jax.random.uniform(k3, (N, N)) < EDGE_P).astype(jnp.float32)
        adj = jnp.maximum(adj, jnp.eye(N, dtype=jnp.float32))
        return {'h': h, 'W': W, 'adj': adj}
    _L0_gnn_all = _L0_gnn_setup()
    _L0_gnn_in = {k: v for k, v in _L0_gnn_all.items() if k in ('W',)}
    del _L0_gnn_all

    def _L1_gnn_setup():
        import jax, jax.numpy as jnp
        import numpy as np
        B, T, D, H = (64, 1024, 128, 128)
        MAX_SKIP = 4

        def _lstm_last(Wih, Whh, bih, bhh, xs):
            N, _, Hd = xs.shape
            bias = bih + bhh

            def step(carry, x_t):
                h, c = carry
                g = x_t @ Wih.T + h @ Whh.T + bias
                i, f, gg, o = jnp.split(g, 4, axis=-1)
                c = jax.nn.sigmoid(f) * c + jax.nn.sigmoid(i) * jnp.tanh(gg)
                h = jax.nn.sigmoid(o) * jnp.tanh(c)
                return ((h, c), None)
            init = (jnp.zeros((N, Hd), xs.dtype), jnp.zeros((N, Hd), xs.dtype))
            (h_last, _), _ = jax.lax.scan(step, init, jnp.swapaxes(xs, 0, 1))
            return h_last
        key = jax.random.key(seed)
        ks = jax.random.split(key, 8)
        s = 0.05
        x = jax.random.normal(ks[0], (B, T, D), jnp.float32)
        adj = jax.random.uniform(ks[1], (T, T), jnp.float32) / T
        Wg0 = jax.random.normal(ks[2], (D, H), jnp.float32) * s
        bg0 = jnp.zeros((H,), jnp.float32)
        Wg1 = jax.random.normal(ks[3], (H, H), jnp.float32) * s
        bg1 = jnp.zeros((H,), jnp.float32)
        Wih = jax.random.normal(ks[4], (MAX_SKIP, 4 * H, H), jnp.float32) * s
        Whh = jax.random.normal(ks[5], (MAX_SKIP, 4 * H, H), jnp.float32) * s
        bih = jax.random.normal(ks[6], (MAX_SKIP, 4 * H), jnp.float32) * s
        bhh = jax.random.normal(ks[7], (MAX_SKIP, 4 * H), jnp.float32) * s
        return dict(x=x, adj=adj, Wg0=Wg0, bg0=bg0, Wg1=Wg1, bg1=bg1, Wih=Wih, Whh=Whh, bih=bih, bhh=bhh)
    _L1_gnn_all = _L1_gnn_setup()
    _L1_gnn_in = {k: v for k, v in _L1_gnn_all.items() if k in ('Wg0', 'bg0', 'Wg1', 'bg1', 'Wih', 'Whh', 'bih', 'bhh')}
    del _L1_gnn_all
    return {'x': x, 'adj': adj, 'L0_gnn_W': _L0_gnn_in['W'], 'L1_gnn_Wg0': _L1_gnn_in['Wg0'], 'L1_gnn_bg0': _L1_gnn_in['bg0'], 'L1_gnn_Wg1': _L1_gnn_in['Wg1'], 'L1_gnn_bg1': _L1_gnn_in['bg1'], 'L1_gnn_Wih': _L1_gnn_in['Wih'], 'L1_gnn_Whh': _L1_gnn_in['Whh'], 'L1_gnn_bih': _L1_gnn_in['bih'], 'L1_gnn_bhh': _L1_gnn_in['bhh']}

def reference(x, adj, L0_gnn_W, L1_gnn_Wg0, L1_gnn_bg0, L1_gnn_Wg1, L1_gnn_bg1, L1_gnn_Wih, L1_gnn_Whh, L1_gnn_bih, L1_gnn_bhh):
    import jax
    import jax.numpy as jnp

    def _L0_gnn_ref(h, W, adj):
        import jax, jax.numpy as jnp
        import numpy as np
        B, N, IN_DIM, OUT_DIM, H = (2, 2048, 128, 128, 4)
        HEAD_DIM = OUT_DIM // H
        EDGE_P = 0.01
        Bn, Nn, _ = h.shape
        qkv = h @ W
        qkv = qkv.reshape(Bn, Nn, 3, H, HEAD_DIM).transpose(2, 0, 3, 1, 4)
        q, k, v = (qkv[0], qkv[1], qkv[2])
        mask = jnp.where(adj == 0, -jnp.inf, 0.0)
        scores = jnp.einsum('bhid,bhjd->bhij', q, k) / np.sqrt(HEAD_DIM) + mask
        attn = jax.nn.softmax(scores, axis=-1)
        out = jnp.einsum('bhij,bhjd->bhid', attn, v)
        return out.transpose(0, 2, 1, 3).reshape(Bn, Nn, OUT_DIM)

    def _L1_gnn_ref(x, adj, Wg0, bg0, Wg1, bg1, Wih, Whh, bih, bhh):
        import jax, jax.numpy as jnp
        import numpy as np
        B, T, D, H = (64, 1024, 128, 128)
        MAX_SKIP = 4

        def _lstm_last(Wih, Whh, bih, bhh, xs):
            N, _, Hd = xs.shape
            bias = bih + bhh

            def step(carry, x_t):
                h, c = carry
                g = x_t @ Wih.T + h @ Whh.T + bias
                i, f, gg, o = jnp.split(g, 4, axis=-1)
                c = jax.nn.sigmoid(f) * c + jax.nn.sigmoid(i) * jnp.tanh(gg)
                h = jax.nn.sigmoid(o) * jnp.tanh(c)
                return ((h, c), None)
            init = (jnp.zeros((N, Hd), xs.dtype), jnp.zeros((N, Hd), xs.dtype))
            (h_last, _), _ = jax.lax.scan(step, init, jnp.swapaxes(xs, 0, 1))
            return h_last
        h = jax.nn.relu(jnp.einsum('ts,bsh->bth', adj, x @ Wg0 + bg0))
        h = jax.nn.relu(jnp.einsum('ts,bsh->bth', adj, h @ Wg1 + bg1))
        Bv, Tv, Hd = h.shape
        for p in range(1, MAX_SKIP + 1):
            nw = Tv // p
            wins = h[:, :nw * p, :].reshape(Bv * nw, p, Hd)
            last = _lstm_last(Wih[p - 1], Whh[p - 1], bih[p - 1], bhh[p - 1], wins)
            idx = jnp.arange(nw) * p + (p - 1)
            h = h.at[:, idx, :].set(last.reshape(Bv, nw, Hd))
        return h
    h = jnp.maximum(_layernorm(x, axis=-1), 0.0)
    x = x + _L0_gnn_ref(h, L0_gnn_W, adj)
    h = jnp.maximum(_layernorm(x, axis=-1), 0.0)
    x = x + _L1_gnn_ref(h, adj, L1_gnn_Wg0, L1_gnn_bg0, L1_gnn_Wg1, L1_gnn_bg1, L1_gnn_Wih, L1_gnn_Whh, L1_gnn_bih, L1_gnn_bhh)
    return x

_drawn_inputs = setup_inputs


def setup_inputs(seed=0):
    import zlib

    import numpy as np

    out = dict(_drawn_inputs(seed))
    spreads = {'L1_gnn_bg0': (0.0, 0.1), 'L1_gnn_bg1': (0.0, 0.446)}
    factors = {'L1_gnn_Whh': 8.0, 'L1_gnn_bih': 3.384, 'L1_gnn_bhh': 3.408}
    for name, (base, spread) in spreads.items():
        noise = np.random.default_rng([zlib.crc32(name.encode()), seed]).standard_normal(out[name].shape)
        drawn = base * np.exp(spread * noise) if base else spread * noise
        out[name] = jnp.asarray(drawn.astype(out[name].dtype))
    for name, factor in factors.items():
        out[name] = (out[name] * factor).astype(out[name].dtype)
    return out
```

```python
from contextlib import ExitStack

import concourse.bass as bass
from concourse import mybir

F32 = mybir.dt.float32
F32R = mybir.dt.float32r
BF16 = mybir.dt.bfloat16
ALU = mybir.AluOpType
ACT = mybir.ActivationFunctionType
AX_X = mybir.AxisListType.X
ds = bass.ds

LN_EPS = 1e-5
MASKED = -1e30
BANK = 512
MAX_SKIP = 4


def gnn_block(
    nc: bass.Bass,
    x: bass.AP,
    adj: bass.AP,
    W_qkv: bass.AP,
    Wg0: bass.AP,
    bg0: bass.AP,
    Wg1: bass.AP,
    bg1: bass.AP,
    Wih: bass.AP,
    Whh: bass.AP,
    bih: bass.AP,
    bhh: bass.AP,
    out: bass.AP,
):
    B, N, D = x.shape
    P = 128
    assert N == P and D == P
    HEADS = 4
    HD = D // HEADS
    SCALE = float(HD) ** -0.5
    GB = BANK // N
    GROUPS = B // GB
    GT = GB * N
    GATES = 4

    SIDE = 4
    STAGES = []
    first = 0
    for p, cb in ((1, 4), (2, 8), (3, 8), (4, 16)):
        rounds = B // cb // SIDE
        STAGES.append((p, cb, rounds, first))
        first += rounds * SIDE * p
    ITEMS = first

    with ExitStack() as ctx:
        def sb(name, shape, dt=F32):
            return ctx.enter_context(nc.sbuf_tensor(name, shape, dt))

        def sem(name):
            return ctx.enter_context(nc.semaphore(name))

        X = sb("X", [P, B, D])
        H_hi = sb("H_hi", [P, B * N], F32R)
        H_lo = sb("H_lo", [P, B * N], F32R)
        W_hi = sb("W_hi", [P, 2, MAX_SKIP, GATES * P], F32R)
        W_lo = sb("W_lo", [P, 2, MAX_SKIP, GATES * P], F32R)
        ident = sb("ident", [P, P])
        ident_bf = sb("ident_bf", [P, P], BF16)
        mask = sb("mask", [P, N], BF16)
        adj_sb = sb("adj_sb", [P, N])
        adjT = sb("adjT", [P, N])
        wqkv = sb("wqkv", [P, 3 * D])
        wg = sb("wg", [P, 2, D])
        bg = sb("bg", [P, 2, D])
        bias_rows = sb("bias_rows", [2 * MAX_SKIP * GATES, P])
        bias_2 = sb("bias_2", [P, 2 * MAX_SKIP * GATES])
        bias = sb("bias", [P, MAX_SKIP * GATES])
        stats = sb("stats", [P, 2, GB, 6])
        mv = sb("mv", [P, 2, GB, 2])
        veps = sb("veps", [P, 2, GB])
        rstd = sb("rstd", [P, 2, GB])
        minus_half = sb("minus_half", [P, GB])
        eps = sb("eps", [P, GB])
        pause = sb("pause", [P, 1])
        released = sb("released", [P, 2])
        rmax = sb("rmax", [P, HEADS * GB])
        rec = sb("rec", [P, GB * HEADS])
        S_hi = sb("S_hi", [P, SIDE, BANK], F32R)
        S_lo = sb("S_lo", [P, SIDE, BANK], F32R)

        arena = sb("arena", [P, 20 * BANK + GB * HEADS])
        at = [0]

        def take(n):
            v = arena[:, at[0]:at[0] + n]
            at[0] += n
            return v

        xn = take(GT).rearrange("p (b d) -> p b d", b=GB)
        xn2 = take(GT).rearrange("p (b d) -> p b d", b=GB)
        hT = take(GT)
        qT = take(GT)
        kT = take(GT)
        v_sb = take(GB * HEADS * (HD + 1)).rearrange("p (b h d) -> p b h d", b=GB, h=HEADS)
        h2T = take(GT)
        h1T = take(GT)
        y_sb = take(GT).rearrange("p (b d) -> p b d", b=GB)
        att = take(GT)
        prob = take(HEADS * GT)
        probT = take(HEADS * GT).rearrange("p (h n) -> p h n", h=HEADS)
        wst = [prob.rearrange("p (c i) -> p c i", i=P), probT.rearrange("p h n -> p (h n)").rearrange("p (c i) -> p c i", i=P)]
        at[0] = 0
        sig_i = take(2 * BANK).rearrange("p (s n) -> p s n", s=2)
        tanh_g = take(2 * BANK).rearrange("p (s n) -> p s n", s=2)
        sig_f = take(2 * BANK).rearrange("p (s n) -> p s n", s=2)
        sig_o = take(SIDE * BANK).rearrange("p (s n) -> p s n", s=SIDE)
        cell = take(SIDE * BANK).rearrange("p (s n) -> p s n", s=SIDE)
        ig = take(2 * BANK).rearrange("p (s n) -> p s n", s=2)
        tanh_c = take(2 * BANK).rearrange("p (s n) -> p s n", s=2)
        h_f = take(2 * BANK).rearrange("p (s n) -> p s n", s=2)
        at[0] = 0
        h_out = take(2 * BANK).rearrange("p (s n) -> p s n", s=2)
        assert at[0] <= 20 * BANK

        ps = ctx.enter_context(nc.psum_tensor("ps", [P, 8, BANK], F32))
        psS = ps[:, 0:HEADS, :]
        psA = ps[:, 4, :]
        psB = ps[:, 5, :]
        psQ = ps[:, 6, :]
        psY = ps[:, 7, :]
        psO = ps[:, 6:8, :]

        x_loaded = sem("x_loaded")
        w_loaded = sem("w_loaded")
        lstm_w_loaded = sem("lstm_w_loaded")
        consts = sem("consts")
        pool_chain = sem("pool_chain")
        wT_done = sem("wT_done")
        w_hi_done = sem("w_hi_done")
        w_lo_done = sem("w_lo_done")
        adjT_done = sem("adjT_done")
        prep_done = sem("prep_done")
        var1 = sem("var1")
        rstd1 = sem("rstd1")
        var2 = sem("var2")
        rstd2 = sem("rstd2")
        veps1 = sem("veps1")
        veps2 = sem("veps2")
        stats1 = sem("stats1")
        stats2 = sem("stats2")
        xn_ready = sem("xn_ready")
        xnT_done = sem("xnT_done")
        hT_ready = sem("hT_ready")
        q_done = sem("q_done")
        q_ready = sem("q_ready")
        k_done = sem("k_done")
        k_ready = sem("k_ready")
        v_done = sem("v_done")
        v_ready = sem("v_ready")
        scores_done = sem("scores_done")
        max_ready = sem("max_ready")
        shifted = sem("shifted")
        exp_ready = sem("exp_ready")
        probT_done = sem("probT_done")
        probT_act = sem("probT_act")
        probT_dve = sem("probT_dve")
        att_done = sem("att_done")
        rec_ready = sem("rec_ready")
        att_read = sem("att_read")
        x2_ready = sem("x2_ready")
        xn2_ready = sem("xn2_ready")
        xn2T_done = sem("xn2T_done")
        h2T_ready = sem("h2T_ready")
        y1_done = sem("y1_done")
        y1_ready = sem("y1_ready")
        z1_done = sem("z1_done")
        h1T_ready = sem("h1T_ready")
        y2_done = sem("y2_done")
        y2_ready = sem("y2_ready")
        z2_done = sem("z2_done")
        H_hi_ready = sem("H_hi_ready")
        H_ready = sem("H_ready")
        gate_sums = sem("gate_sums")
        gate_acts = sem("gate_acts")
        ig_ready = sem("ig_ready")
        fc_ready = sem("fc_ready")
        cells = sem("cells")
        tanhs = sem("tanhs")
        h_f_ready = sem("h_f_ready")
        s_hi_ready = sem("s_hi_ready")
        steps = sem("steps")
        h_sum = sem("h_sum")
        hT_out = sem("hT_out")
        out_ready = sem("out_ready")
        out_stored = sem("out_stored")

        block = ctx.enter_context(nc.Block())

        def tokens(T, chunk, p, cb, t):
            v = T[:, ds(chunk * (cb * N), cb * N)].rearrange("k (b n) -> k b n", n=N)
            return v[:, :, 0:N // p * p].rearrange("k b (w q) -> k b w q", q=p)[:, :, :, t]

        def width(p, cb):
            return cb * (N // p)

        def pipeline(eng, iteration):
            iteration(0, True, False, False)
            iteration(1, True, True, False)
            with eng.Fori(2, GROUPS - 1) as k:
                iteration(k, True, True, True)
            iteration(GROUPS - 1, True, True, True, last=True)
            iteration(GROUPS, False, True, True)
            iteration(GROUPS + 1, False, False, True)

        @block.sync
        def _(sp):
            sp.dma_start(adj_sb[:], adj).then_inc(w_loaded, 16)
            sp.dma_start(wqkv[:], W_qkv).then_inc(w_loaded, 16)
            sp.dma_start(X[:, 0:GB, :], x[0:GB, :, :].rearrange("b n d -> n b d")).then_inc(x_loaded, 16)
            with sp.Fori(1, GROUPS) as g:
                sp.wait_ge(x_loaded, g * 16)
                sp.dma_start(X[:, ds(g * GB, GB), :],
                             x[ds(g * GB, GB), :, :].rearrange("b n d -> n b d")).then_inc(x_loaded, 16)
            with sp.Fori(0, GROUPS) as g:
                sp.wait_ge(out_ready, g + 1)
                sp.dma_start(out[ds(g * GB, GB), :, :].rearrange("b n d -> n b d"),
                             X[:, ds(g * GB, GB), :]).then_inc(out_stored, 16)
            sp.wait_ge(out_stored, 16 * GROUPS)

        @block.gpsimd
        def _(pool):
            g_ = nc.gpsimd
            g_.memset(minus_half[:], -0.5)
            g_.memset(eps[:], LN_EPS)
            g_.memset(ident[:], 0.0)
            g_.memset(v_sb[:, :, :, HD:HD + 1], 1.0).then_inc(pool_chain, 1)
            pool.wait_ge(pool_chain, 1)
            g_.affine_select(out=ident[:], in_=ident[:], compare_op=ALU.not_equal, fill=1.0, base=0,
                             pattern=[[-1, P]], channel_multiplier=1).then_inc(pool_chain, 1)
            pool.wait_ge(pool_chain, 2)
            g_.tensor_copy(ident_bf[:], ident[:]).then_inc(consts, 1)

            def rsqrt(layer, g, var, ve, done):
                pool.wait_ge(var, g + 1)
                g_.tensor_tensor(veps[:, layer, :], mv[:, layer, :, 1], eps[:], ALU.add).then_inc(ve, 1)
                pool.wait_ge(ve, g + 1)
                g_.tensor_tensor(rstd[:, layer, :], veps[:, layer, :], minus_half[:], ALU.pow).then_inc(done, 1)

            rsqrt(0, 0, var1, veps1, rstd1)

            def iteration(k, front, mid, back, last=False):
                if front and not last:
                    rsqrt(0, k + 1, var1, veps1, rstd1)
                if mid:
                    rsqrt(1, k - 1, var2, veps2, rstd2)

            pipeline(pool, iteration)

            done = 0
            for p, cb, rounds, first in STAGES:
                n_cols = width(p, cb)
                if p == 1:
                    continue
                with pool.Fori(0, rounds) as r:
                    for t in range(1, p):
                        for c in range(SIDE):
                            n = r * (SIDE * p) + (first + t * SIDE + c)
                            pool.wait_ge(gate_acts, n * 4 + (8 + 2))
                            pool.wait_ge(cells, n + 1)
                            g_.tensor_tensor(ig[:, c % 2, 0:n_cols], sig_i[:, c % 2, 0:n_cols],
                                             tanh_g[:, c % 2, 0:n_cols], ALU.mult).then_inc(ig_ready, 1)

        @block.scalar
        def _(act):
            a_ = nc.scalar
            act.dma_start(wg[:, 0, :], Wg0).then_inc(w_loaded, 16)
            act.dma_start(wg[:, 1, :], Wg1).then_inc(w_loaded, 16)
            act.dma_start(bg[:, 0, :], bg0.partition_broadcast(P)).then_inc(w_loaded, 16)
            act.dma_start(bg[:, 1, :], bg1.partition_broadcast(P)).then_inc(w_loaded, 16)
            act.dma_start(bias_rows[0:16, :], bih.rearrange("p (c j) -> (p c) j", j=P)).then_inc(w_loaded, 16)
            act.dma_start(bias_rows[16:32, :], bhh.rearrange("p (c j) -> (p c) j", j=P)).then_inc(w_loaded, 16)
            act.dma_start(wst[0], Wih.rearrange("p (c j) i -> j (p c) i", j=P)).then_inc(lstm_w_loaded, 16)
            act.dma_start(wst[1], Whh.rearrange("p (c j) i -> j (p c) i", j=P)).then_inc(lstm_w_loaded, 16)
            for m in range(2 * MAX_SKIP):
                act.wait_ge(wT_done, m + 1)
                a_.activation(W_hi[:, m // MAX_SKIP, m % MAX_SKIP, :], ps[:, m, :], ACT.Copy).then_inc(w_hi_done, 1)

            def iteration(k, front, mid, back, last=False):
                if front:
                    act.wait_ge(xnT_done, k + 1)
                    a_.activation(hT[:], psA, ACT.Relu).then_inc(hT_ready, 1)
                if back:
                    act.wait_ge(xn2T_done, k - 1)
                    a_.activation(h2T[:], psB, ACT.Relu).then_inc(h2T_ready, 1)
                if front:
                    act.wait_ge(q_done, k + 1)
                    a_.activation(qT[:], psQ, ACT.Copy).then_inc(q_ready, 1)
                if back:
                    act.wait_ge(z1_done, k - 1)
                    a_.activation(h1T[:], psB, ACT.Relu).then_inc(h1T_ready, 1)
                if front:
                    act.wait_ge(k_done, k + 1)
                    a_.activation(kT[:], psQ, ACT.Copy).then_inc(k_ready, 1)
                if mid:
                    act.wait_ge(shifted, k)
                    a_.activation(prob[:], prob[:], ACT.Exp, scale=SCALE).then_inc(exp_ready, 1)
                    act.wait_ge(probT_done, k * 2 - 1)
                    a_.activation(probT[:, 0:2, :], psS[:, 0:2, :], ACT.Copy).then_inc(probT_act, 1)
                if back:
                    act.wait_ge(z2_done, k - 1)
                    a_.activation(H_hi[:, ds(k * GT - 2 * GT, GT)], psB, ACT.Relu).then_inc(H_hi_ready, 1)

            pipeline(act, iteration)

            act.wait_ge(H_ready, GROUPS)
            act.wait_ge(att_read, GROUPS)
            act.wait_ge(x2_ready, GROUPS)
            a_.activation(sig_i[:, 0, 0:1], bias[:, 0:1], ACT.Sigmoid).then_inc(gate_acts, 8)

            for p, cb, rounds, first in STAGES:
                n_cols = width(p, cb)
                with act.Fori(0, rounds) as r:
                    def gates(t, c):
                        n = r * (SIDE * p) + (first + t * SIDE + c)
                        for j, (gate, func, to) in enumerate((
                                (0, ACT.Sigmoid, sig_i[:, c % 2, 0:n_cols]), (2, ACT.Tanh, tanh_g[:, c % 2, 0:n_cols]),
                                (1, ACT.Sigmoid, sig_f[:, c % 2, 0:n_cols]), (3, ACT.Sigmoid, sig_o[:, c, 0:n_cols]))):
                            if t == 0 and gate == 1:
                                continue
                            if j == 0:
                                act.wait_ge(cells, n + 1)
                            if j == 3:
                                act.wait_ge(h_f_ready, n + 1)
                            act.wait_ge(gate_sums, n * 4 + (j + 1))
                            a_.activation(to, ps[:, 4 * (c % 2) + j, 0:n_cols], func,
                                          bias=bias[:, GATES * (p - 1) + gate:GATES * (p - 1) + gate + 1])\
                                .then_inc(gate_acts, 2 if t == 0 and j == 1 else 1)

                    def tanh(t, c):
                        n = r * (SIDE * p) + (first + t * SIDE + c)
                        act.wait_ge(cells, n + (2 + 1))
                        act.wait_ge(h_f_ready, n + 3)
                        a_.activation(tanh_c[:, c % 2, 0:n_cols], cell[:, c, 0:n_cols], ACT.Tanh).then_inc(tanhs, 1)

                    order = [(t, c) for t in range(p) for c in range(SIDE)]
                    for m, item in enumerate(order):
                        gates(*item)
                        if m:
                            tanh(*order[m - 1])
                    tanh(*order[-1])

        @block.tensor
        def _(pe):
            mm = nc.tensor.matmul

            def transposed(to, src, n=GB):
                for b in range(n):
                    last = nc.tensor.transpose(to[:, b * P:(b + 1) * P], src[:, b, :], ident[:])
                return last

            pe.wait_ge(consts, 1)
            pe.wait_ge(lstm_w_loaded, 32)
            for m in range(2 * MAX_SKIP):
                w = wst[m // MAX_SKIP][:, GATES * (m % MAX_SKIP):GATES * (m % MAX_SKIP + 1), :]
                transposed(ps[:, m, :], w, GATES).then_inc(wT_done, 1)
            pe.wait_ge(w_loaded, 16 * 8)
            pe.wait_ge(w_lo_done, 1)
            nc.tensor.transpose(ps[:, 0, 0:P], adj_sb[:], ident[:])
            nc.tensor.transpose(ps[:, 0, P:P + 32], bias_rows[:], ident[0:32, 0:32]).then_inc(adjT_done, 1)
            pe.wait_ge(prep_done, 1)

            def iteration(k, front, mid, back, last=False):
                if front:
                    pe.wait_ge(xn_ready, k + 1)
                    if not (isinstance(k, int) and k == 0):
                        pe.wait_ge(v_ready, k)
                    transposed(psA, xn).then_inc(xnT_done, 1)
                if back:
                    pe.wait_ge(xn2_ready, k - 1)
                    if not (isinstance(k, int) and k == 2):
                        pe.wait_ge(H_ready, k - 2)
                    transposed(psB, xn2).then_inc(xn2T_done, 1)
                if front:
                    pe.wait_ge(hT_ready, k + 1)
                    if mid and not (isinstance(k, int) and k == 1):
                        pe.wait_ge(att_read, k - 1)
                    mm(psQ, wqkv[:, 0:D], hT[:], start=True, stop=True).then_inc(q_done, 1)
                if back:
                    pe.wait_ge(h2T_ready, k - 1)
                    pe.wait_ge(att_read, k - 1)
                    for b in range(GB):
                        l = mm(psY[:, b * D:(b + 1) * D], h2T[:, b * N:(b + 1) * N], wg[:, 0, :], start=True, stop=True)
                    l.then_inc(y1_done, 1)
                if front:
                    for b in range(GB):
                        l = mm(psA[:, b * D:(b + 1) * D], hT[:, b * N:(b + 1) * N], wqkv[:, 2 * D:3 * D],
                               start=True, stop=True)
                    l.then_inc(v_done, 1)
                if back:
                    pe.wait_ge(y1_ready, k - 1)
                    for b in range(GB):
                        l = mm(psB[:, b * N:(b + 1) * N], y_sb[:, b, :], adjT[:], start=True, stop=True)
                    l.then_inc(z1_done, 1)
                if front:
                    pe.wait_ge(q_ready, k + 1)
                    mm(psQ, wqkv[:, D:2 * D], hT[:], start=True, stop=True).then_inc(k_done, 1)
                if back:
                    pe.wait_ge(h1T_ready, k - 1)
                    for b in range(GB):
                        l = mm(psY[:, b * D:(b + 1) * D], h1T[:, b * N:(b + 1) * N], wg[:, 1, :], start=True, stop=True)
                    l.then_inc(y2_done, 1)
                if mid:
                    pe.wait_ge(exp_ready, k)
                    pv = prob.rearrange("p (h b n) -> p h b n", h=HEADS, b=GB)
                    for h in range(HEADS):
                        l = transposed(psS[:, h, :], pv[:, h, :, :])
                        if h % 2:
                            l.then_inc(probT_done, 1)
                if back:
                    pe.wait_ge(y2_ready, k - 1)
                    for b in range(GB):
                        l = mm(psB[:, b * N:(b + 1) * N], y_sb[:, b, :], adjT[:], start=True, stop=True)
                    l.then_inc(z2_done, 1)
                if mid:
                    if front:
                        pe.wait_ge(k_ready, k + 1)
                    pe.wait_ge(probT_act, k)
                    pe.wait_ge(probT_dve, k)
                    for b in range(GB):
                        for h in range(HEADS):
                            o = (b % 2) * HEADS + h
                            l = mm(psO[:, b // 2, o * (HD + 1):(o + 1) * (HD + 1)],
                                   probT[:, h, b * N:(b + 1) * N], v_sb[:, b, h, :], start=True, stop=True)
                    l.then_inc(att_done, 1)
                if front:
                    pe.wait_ge(k_ready, k + 1)
                    for h in range(HEADS):
                        mm(psS[:, h, :].rearrange("p (b n) -> p b n", n=N), ident_bf[:],
                           mask[:].unsqueeze(1).to_broadcast([P, GB, N]), start=True, stop=False)
                    for b in range(GB):
                        for h in range(HEADS):
                            l = mm(psS[:, h, b * N:(b + 1) * N], qT[h * HD:(h + 1) * HD, b * N:(b + 1) * N],
                                   kT[h * HD:(h + 1) * HD, b * N:(b + 1) * N], start=False, stop=b == GB - 1)
                    l.then_inc(scores_done, 1)

            pipeline(pe, iteration)

            for s, (p, cb, rounds, first) in enumerate(STAGES):
                n_cols = width(p, cb)
                if p == 1:
                    pe.wait_ge(H_ready, GROUPS)
                with pe.Fori(0, rounds) as r:
                    for t in range(p):
                        for c in range(SIDE):
                            n = r * (SIDE * p) + (first + t * SIDE + c)
                            chunk = r * SIDE + c
                            if t:
                                pe.wait_ge(steps, n - 3)
                            elif p > 1:
                                p0, cb0, rounds0, first0 = STAGES[s - 1]
                                ratio = cb // cb0
                                lastc = ratio * c + ratio - 1
                                whole, part = lastc // SIDE, lastc % SIDE
                                pe.wait_ge(steps, r * (ratio * SIDE * p0)
                                           + (first0 + whole * SIDE * p0 + (p0 - 1) * SIDE + part + 1))
                            x_hi, x_lo = tokens(H_hi, chunk, p, cb, t), tokens(H_lo, chunk, p, cb, t)
                            for j, gate in enumerate((0, 2, 1, 3)):
                                if t == 0 and gate == 1:
                                    continue
                                pe.wait_ge(gate_acts, n * 4 + (j + 1))
                                to = ps[:, 4 * (c % 2) + j, 0:n_cols]
                                to3 = to.rearrange("k (b w) -> k b w", b=cb)
                                wi = slice(gate * P, (gate + 1) * P)
                                terms = [(to3, W_hi[:, 0, p - 1, wi], x_hi), (to3, W_hi[:, 0, p - 1, wi], x_lo),
                                         (to3, W_lo[:, 0, p - 1, wi], x_hi)]
                                if t:
                                    s_hi, s_lo = S_hi[:, c, 0:n_cols], S_lo[:, c, 0:n_cols]
                                    terms += [(to, W_hi[:, 1, p - 1, wi], s_hi), (to, W_hi[:, 1, p - 1, wi], s_lo),
                                              (to, W_lo[:, 1, p - 1, wi], s_hi)]
                                for m, (o, w, v) in enumerate(terms):
                                    l = mm(o, w, v, start=m == 0, stop=m == len(terms) - 1)
                                l.then_inc(gate_sums, 2 if t == 0 and j == 1 else 1)

            with pe.Fori(0, GROUPS // 2) as r:
                for u in range(2):
                    pe.wait_ge(h_sum, r * 2 + (u + 1))
                    transposed(ps[:, u, :], h_out[:, u, :].rearrange("p (b n) -> p b n", b=GB)).then_inc(hT_out, 1)

        @block.vector
        def _(dve):
            v_ = nc.vector
            for m in range(2 * MAX_SKIP):
                dve.wait_ge(w_hi_done, m + 1)
                v_.tensor_tensor(W_lo[:, m // MAX_SKIP, m % MAX_SKIP, :], ps[:, m, :],
                                 W_hi[:, m // MAX_SKIP, m % MAX_SKIP, :].bitcast(F32), ALU.subtract).then_inc(w_lo_done, 1)
            dve.wait_ge(adjT_done, 1)
            v_.tensor_copy(adjT[:], ps[:, 0, 0:P])
            v_.tensor_copy(bias_2[:], ps[:, 0, P:P + 32]).then_inc(prep_done, 1)
            v_.tensor_scalar(mask[:], adj_sb[:], 0.0, MASKED, ALU.is_equal, ALU.mult)
            dve.wait_ge(prep_done, 1)
            v_.tensor_tensor(bias[:], bias_2[:, 0:16], bias_2[:, 16:32], ALU.add)

            def moments(layer, g, stats_ready, var):
                for b in range(GB):
                    l = v_.bn_stats(stats[:, layer, b, :], X[:, ds(g * GB + b, 1), :].rearrange("p a d -> p (a d)"))
                l.then_inc(stats_ready, 1)
                dve.wait_ge(stats_ready, g + 1)
                v_.memset(pause[:], 0.0)
                for b in range(GB):
                    l = v_.bn_aggr(mv[:, layer, b, :], stats[:, layer, b, :])
                l.then_inc(var, 1)

            def normalize(layer, g, to, rstd_ready, ready):
                dve.wait_ge(rstd_ready, g + 1)
                for b in range(GB):
                    l = v_.tensor_scalar(to[:, b, :], X[:, ds(g * GB + b, 1), :].rearrange("p a d -> p (a d)"),
                                         mv[:, layer, b, 0:1], rstd[:, layer, b:b + 1], ALU.subtract, ALU.mult)
                l.then_inc(ready, 1)

            dve.wait_ge(x_loaded, 16)
            moments(0, 0, stats1, var1)
            normalize(0, 0, xn, rstd1, xn_ready)
            y_bias = [bg[:, i, :].unsqueeze(1).to_broadcast([P, GB, D]) for i in range(2)]
            psY3 = psY.rearrange("p (b d) -> p b d", d=D)

            def iteration(k, front, mid, back, last=False):
                if mid:
                    dve.wait_ge(scores_done, k)
                    s3 = psS.rearrange("p h (b n) -> p (h b) n", n=N)
                    v_.tensor_reduce(rmax[:], s3, AX_X, ALU.max).then_inc(max_ready, 1)
                if front and not last:
                    dve.wait_ge(x_loaded, k * 16 + 32)
                    moments(0, k + 1, stats1, var1)
                if back:
                    dve.wait_ge(y1_done, k - 1)
                    v_.tensor_tensor(y_sb, psY3, y_bias[0], ALU.add).then_inc(y1_ready, 1)
                if mid:
                    dve.wait_ge(max_ready, k)
                    v_.tensor_tensor(prob.rearrange("p (c n) -> p c n", n=N), s3,
                                     rmax[:].unsqueeze(2).to_broadcast([P, HEADS * GB, N]), ALU.subtract)\
                        .then_inc(shifted, 1)
                if back:
                    dve.wait_ge(y2_done, k - 1)
                    v_.tensor_tensor(y_sb, psY3, y_bias[1], ALU.add).then_inc(y2_ready, 1)
                if front and not last:
                    dve.wait_ge(xnT_done, k + 1)
                    normalize(0, k + 1, xn, rstd1, xn_ready)
                if mid:
                    dve.wait_ge(probT_done, k * 2)
                    v_.tensor_copy(probT[:, 2:4, :], psS[:, 2:4, :]).then_inc(probT_dve, 1)
                if back:
                    dve.wait_ge(H_hi_ready, k - 1)
                    at_ = ds(k * GT - 2 * GT, GT)
                    v_.scalar_tensor_tensor(H_lo[:, at_], psB, 0.0, H_hi[:, at_].bitcast(F32),
                                            ALU.max, ALU.subtract).then_inc(H_ready, 1)
                if mid:
                    dve.wait_ge(att_done, k)
                    o4 = psO[:, :, 0:2 * HEADS * (HD + 1)].rearrange("p a (c d) -> p a c d", d=HD + 1)
                    r3 = rec[:].rearrange("p (a c) -> p a c", a=2)
                    v_.reciprocal(r3, o4[:, :, :, HD]).then_inc(rec_ready, 1)
                if front:
                    dve.wait_ge(v_done, k + 1)
                    v_.tensor_copy(v_sb[:, :, :, 0:HD], psA.rearrange("p (b h d) -> p b h d", b=GB, h=HEADS))\
                        .then_inc(v_ready, 1)
                if mid:
                    dve.wait_ge(rec_ready, k)
                    v_.tensor_tensor(att.rearrange("p (a c d) -> p a c d", a=2, d=HD), o4[:, :, :, 0:HD],
                                     r3.unsqueeze(3).to_broadcast([P, 2, 2 * HEADS, HD]), ALU.mult).then_inc(att_read, 1)
                    dve.wait_ge(att_read, k)
                    xg = X[:, ds(k * GB - GB, GB), :]
                    v_.tensor_tensor(xg, xg, att.rearrange("p (b d) -> p b d", b=GB), ALU.add).then_inc(x2_ready, 1)
                    dve.wait_ge(x2_ready, k)
                    moments(1, k - 1, stats2, var2)
                    normalize(1, k - 1, xn2, rstd2, xn2_ready)

            pipeline(dve, iteration)

            dve.wait_ge(gate_acts, 8)
            v_.memset(released[:, 0:1], 0.0).then_inc(cells, 2)
            v_.memset(released[:, 1:2], 0.0).then_inc(h_f_ready, 4)
            later = 0
            for p, cb, rounds, first in STAGES:
                n_cols = width(p, cb)
                with dve.Fori(0, rounds) as r:
                    def cell_part(t, c):
                        n = r * (SIDE * p) + (first + t * SIDE + c)
                        dve.wait_ge(gate_acts, n * 4 + (8 + 2 if t == 0 else 8 + 3))
                        if t == 0:
                            v_.tensor_tensor(cell[:, c, 0:n_cols], sig_i[:, c % 2, 0:n_cols],
                                             tanh_g[:, c % 2, 0:n_cols], ALU.mult).then_inc(cells, 1)
                            return
                        m = r * (SIDE * (p - 1)) + (later + (t - 1) * SIDE + c + 1)
                        v_.tensor_tensor(cell[:, c, 0:n_cols], sig_f[:, c % 2, 0:n_cols],
                                         cell[:, c, 0:n_cols], ALU.mult).then_inc(fc_ready, 1)
                        dve.wait_ge(fc_ready, m)
                        dve.wait_ge(ig_ready, m)
                        v_.tensor_tensor(cell[:, c, 0:n_cols], cell[:, c, 0:n_cols],
                                         ig[:, c % 2, 0:n_cols], ALU.add).then_inc(cells, 1)

                    def state_part(t, c):
                        n = r * (SIDE * p) + (first + t * SIDE + c)
                        chunk = r * SIDE + c
                        dve.wait_ge(gate_acts, n * 4 + (8 + 4))
                        dve.wait_ge(tanhs, n + 1)
                        if t == p - 1:
                            hi, lo = tokens(H_hi, chunk, p, cb, t), tokens(H_lo, chunk, p, cb, t)
                        else:
                            hi, lo = S_hi[:, c, 0:n_cols], S_lo[:, c, 0:n_cols]
                        h = h_f[:, c % 2, 0:n_cols]
                        v_.tensor_tensor(h, sig_o[:, c, 0:n_cols], tanh_c[:, c % 2, 0:n_cols], ALU.mult)\
                            .then_inc(h_f_ready, 1)
                        if t == p - 1:
                            h = h.rearrange("k (b w) -> k b w", b=cb)
                        dve.wait_ge(h_f_ready, n + (4 + 1))
                        v_.tensor_copy(hi, h).then_inc(s_hi_ready, 1)
                        dve.wait_ge(s_hi_ready, n + 1)
                        v_.tensor_tensor(lo, h, hi.bitcast(F32), ALU.subtract).then_inc(steps, 1)

                    order = [(t, c) for t in range(p) for c in range(SIDE)]
                    for m, item in enumerate(order):
                        cell_part(*item)
                        if m:
                            state_part(*order[m - 1])
                    state_part(*order[-1])
                later += rounds * SIDE * (p - 1)

            dve.wait_ge(steps, ITEMS)

            def h_whole(g, u):
                v_.tensor_tensor(h_out[:, u, :], H_hi[:, ds(g * GT, GT)].bitcast(F32),
                                 H_lo[:, ds(g * GT, GT)].bitcast(F32), ALU.add).then_inc(h_sum, 1)

            with dve.Fori(0, GROUPS // 2) as r:
                for u in range(2):
                    h_whole(r * 2 + u, u)
                for u in range(2):
                    g = r * 2 + u
                    dve.wait_ge(hT_out, g + 1)
                    xg = X[:, ds(g * GB, GB), :]
                    v_.tensor_tensor(xg, xg, ps[:, u, :].rearrange("p (b d) -> p b d", b=GB), ALU.add)\
                        .then_inc(out_ready, 1)


_INS = ['x', 'adj', 'L0_gnn_W', 'L1_gnn_Wg0', 'L1_gnn_bg0', 'L1_gnn_Wg1', 'L1_gnn_bg1', 'L1_gnn_Wih', 'L1_gnn_Whh',
        'L1_gnn_bih', 'L1_gnn_bhh']


def kernel(**inputs):
    import numpy as _np
    import concourse.bacc as _bacc
    from concourse import mybir as _mybir
    from concourse.bass_utils import run_bass_kernel_spmd as _run

    nc = _bacc.Bacc("TRN2", target_bir_lowering=False, num_devices=1)
    arrays, args = {}, []
    for name in _INS:
        a = _np.ascontiguousarray(inputs[name])
        arrays[f"in_{name}_dram"] = a
        args.append(nc.dram_tensor(f"in_{name}_dram", a.shape, _mybir.dt.from_np(a.dtype), kind="ExternalInput").ap())
    shape = inputs['x'].shape
    args.append(nc.dram_tensor("out_0_dram", shape, _mybir.dt.float32, kind="ExternalOutput").ap())
    gnn_block(nc, *args)
    r = _run(nc, [arrays], core_ids=[0])
    return r.results[0]["out_0_dram"]
```

```python
from contextlib import ExitStack

import concourse.bass as bass
from concourse import mybir

F32 = mybir.dt.float32
F32R = mybir.dt.float32r
BF16 = mybir.dt.bfloat16
ALU = mybir.AluOpType
ACT = mybir.ActivationFunctionType
AX_X = mybir.AxisListType.X
ds = bass.ds

LN_EPS = 1e-5
MASKED = -1e30
BANK = 512
MAX_SKIP = 4


def gnn_block(
    nc: bass.Bass,
    x: bass.AP,
    adj: bass.AP,
    W_qkv: bass.AP,
    Wg0: bass.AP,
    bg0: bass.AP,
    Wg1: bass.AP,
    bg1: bass.AP,
    Wih: bass.AP,
    Whh: bass.AP,
    bih: bass.AP,
    bhh: bass.AP,
    out: bass.AP,
):
    B, N, D = x.shape
    P = 128
    assert N == P and D == P
    HEADS = 4
    HD = D // HEADS
    SCALE = float(HD) ** -0.5
    GB = BANK // N
    GROUPS = B // GB
    GT = GB * N
    GATES = 4

    SIDE = 4
    STAGES = []
    first = 0
    for p, cb in ((1, 4), (2, 8), (3, 8), (4, 16)):
        rounds = B // cb // SIDE
        STAGES.append((p, cb, rounds, first))
        first += rounds * SIDE * p
    ITEMS = first

    with ExitStack() as ctx:
        def sb(name, shape, dt=F32):
            return ctx.enter_context(nc.sbuf_tensor(name, shape, dt))

        def sem(name):
            return ctx.enter_context(nc.semaphore(name))

        X = sb("X", [P, B, D])
        H_hi = sb("H_hi", [P, B * N], F32R)
        H_lo = sb("H_lo", [P, B * N], F32R)
        W_hi = sb("W_hi", [P, 2, MAX_SKIP, GATES * P], F32R)
        W_lo = sb("W_lo", [P, 2, MAX_SKIP, GATES * P], F32R)
        ident = sb("ident", [P, P])
        ident_bf = sb("ident_bf", [P, P], BF16)
        mask = sb("mask", [P, N], BF16)
        adj_sb = sb("adj_sb", [P, N])
        adjT = sb("adjT", [P, N])
        wqkv = sb("wqkv", [P, 3 * D])
        wg = sb("wg", [P, 2, D])
        bg_rows = sb("bg_rows", [1, 2, D])
        bg_f = sb("bg_f", [1, 2, GB, D])
        bg_hi = sb("bg_hi", [1, 2, GB, D], F32R)
        bg_lo = sb("bg_lo", [1, 2, GB, D], F32R)
        ones_row = sb("ones_row", [1, P], F32R)
        ones_f = sb("ones_f", [1, P])
        bias_rows = sb("bias_rows", [2 * MAX_SKIP * GATES, P])
        bias_2 = sb("bias_2", [P, 2 * MAX_SKIP * GATES])
        bias = sb("bias", [P, MAX_SKIP * GATES])
        stats = sb("stats", [P, 2, GB, 6])
        mv = sb("mv", [P, 2, GB, 2])
        veps = sb("veps", [P, 2, GB])
        rstd = sb("rstd", [P, 2, GB])
        minus_half = sb("minus_half", [P, GB])
        eps = sb("eps", [P, GB])
        pause = sb("pause", [P, 1])
        released = sb("released", [P, 2])
        rmax = sb("rmax", [P, HEADS * GB])
        rec = sb("rec", [P, GB * HEADS])
        S_hi = sb("S_hi", [P, SIDE, BANK], F32R)
        S_lo = sb("S_lo", [P, SIDE, BANK], F32R)

        arena = sb("arena", [P, 21 * BANK + 2 * GB * HEADS])
        at = [0]

        def take(n):
            v = arena[:, at[0]:at[0] + n]
            at[0] += n
            return v

        xn = take(GT).rearrange("p (b d) -> p b d", b=GB)
        xn2 = take(GT).rearrange("p (b d) -> p b d", b=GB)
        hT = take(GT)
        qT = take(GT)
        kT = take(GT)
        v_sb = take(2 * GB * HEADS * (HD + 1)).rearrange("p (s b h d) -> p s b h d", s=2, b=GB, h=HEADS)
        h2T = take(GT)
        h1T = take(GT)
        y_flat = take(GT)
        y_sb = y_flat.rearrange("p (b d) -> p b d", b=GB)
        att = take(GT)
        prob = take(HEADS * GT)
        probT = take(HEADS * GT).rearrange("p (h n) -> p h n", h=HEADS)
        C = MAX_SKIP * GATES
        wst = [X[:, B - 2 * C:B - C, :], X[:, B - C:B, :]]
        EARLY = (B - 2 * C) // GB
        at[0] = 0
        sig_i = take(2 * BANK).rearrange("p (s n) -> p s n", s=2)
        tanh_g = take(2 * BANK).rearrange("p (s n) -> p s n", s=2)
        sig_f = take(2 * BANK).rearrange("p (s n) -> p s n", s=2)
        sig_o = take(SIDE * BANK).rearrange("p (s n) -> p s n", s=SIDE)
        cell = take(SIDE * BANK).rearrange("p (s n) -> p s n", s=SIDE)
        ig = take(2 * BANK).rearrange("p (s n) -> p s n", s=2)
        tanh_c = take(2 * BANK).rearrange("p (s n) -> p s n", s=2)
        h_f = take(2 * BANK).rearrange("p (s n) -> p s n", s=2)
        at[0] = 0
        h_out = take(2 * BANK).rearrange("p (s n) -> p s n", s=2)
        assert at[0] <= 21 * BANK

        ps = ctx.enter_context(nc.psum_tensor("ps", [P, 8, BANK], F32))
        psS = ps[:, 0:HEADS, :]
        psA = ps[:, 4, :]
        psB = ps[:, 5, :]
        psQ = ps[:, 6, :]
        psK = ps[:, 7, :]
        psO = ps[:, 6:8, :]

        x_loaded = sem("x_loaded")
        w_loaded = sem("w_loaded")
        lstm_w_loaded = sem("lstm_w_loaded")
        bg_loaded = sem("bg_loaded")
        bg_copied = sem("bg_copied")
        bg_hi_ready = sem("bg_hi_ready")
        bg_ready = sem("bg_ready")
        consts = sem("consts")
        pool_chain = sem("pool_chain")
        wT_done = sem("wT_done")
        w_hi_done = sem("w_hi_done")
        w_lo_done = sem("w_lo_done")
        adjT_done = sem("adjT_done")
        prep_done = sem("prep_done")
        var1 = sem("var1")
        rstd1 = sem("rstd1")
        var2 = sem("var2")
        rstd2 = sem("rstd2")
        veps1 = sem("veps1")
        veps2 = sem("veps2")
        stats1 = sem("stats1")
        stats2 = sem("stats2")
        xn_ready = sem("xn_ready")
        xnT_done = sem("xnT_done")
        hT_ready = sem("hT_ready")
        q_done = sem("q_done")
        q_ready = sem("q_ready")
        k_done = sem("k_done")
        k_ready = sem("k_ready")
        v_done = sem("v_done")
        v_ready = sem("v_ready")
        scores_done = sem("scores_done")
        max_ready = sem("max_ready")
        shifted = sem("shifted")
        exp_ready = sem("exp_ready")
        probT_done = sem("probT_done")
        probT_ready = sem("probT_ready")
        att_done = sem("att_done")
        rec_ready = sem("rec_ready")
        att_read = sem("att_read")
        x2_ready = sem("x2_ready")
        xn2_ready = sem("xn2_ready")
        xn2T_done = sem("xn2T_done")
        h2T_ready = sem("h2T_ready")
        y1_done = sem("y1_done")
        y1_ready = sem("y1_ready")
        z1_done = sem("z1_done")
        h1T_ready = sem("h1T_ready")
        y2_done = sem("y2_done")
        y2_ready = sem("y2_ready")
        z2_done = sem("z2_done")
        H_hi_ready = sem("H_hi_ready")
        H_ready = sem("H_ready")
        gate_sums = sem("gate_sums")
        gate_acts = sem("gate_acts")
        ig_ready = sem("ig_ready")
        fc_ready = sem("fc_ready")
        cells = sem("cells")
        tanhs = sem("tanhs")
        h_f_ready = sem("h_f_ready")
        s_hi_ready = sem("s_hi_ready")
        steps = sem("steps")
        h_sum = sem("h_sum")
        hT_out = sem("hT_out")
        out_ready = sem("out_ready")
        out_stored = sem("out_stored")

        block = ctx.enter_context(nc.Block())

        def tokens(T, chunk, p, cb, t):
            v = T[:, ds(chunk * (cb * N), cb * N)].rearrange("k (b n) -> k b n", n=N)
            return v[:, :, 0:N // p * p].rearrange("k b (w q) -> k b w q", q=p)[:, :, :, t]

        def width(p, cb):
            return cb * (N // p)

        class Step:

            def __init__(self, k, at=None):
                at = k if at is None else at
                self.k, self.par, self.at = k, at % 2, at
                self.front, self.mid, self.back = at < GROUPS, 1 <= at <= GROUPS, 2 <= at
                self.next1, self.next2 = at + 1 < GROUPS, at + 2 < GROUPS
                self.prep = at == 1

        def pipeline(eng, iteration):
            iteration(Step(0))
            iteration(Step(1))
            iteration(Step(2))
            iteration(Step(3))
            with eng.Fori(0, (GROUPS - 6) // 2) as r:
                iteration(Step(r * 2 + 4, 4))
                iteration(Step(r * 2 + 5, 5))
            for k in range(GROUPS - 2, GROUPS + 2):
                iteration(Step(k))

        @block.sync
        def _(sp):
            def load(g):
                sp.dma_start(X[:, ds(g * GB, GB), :],
                             x[ds(g * GB, GB), :, :].rearrange("b n d -> n b d")).then_inc(x_loaded, 16)

            load(0)
            sp.dma_start(adj_sb[:], adj).then_inc(w_loaded, 16)
            sp.dma_start(bg_rows[:, 0, :], bg0.rearrange("(a n) -> a n", a=1)).then_inc(bg_loaded, 16)
            sp.dma_start(bg_rows[:, 1, :], bg1.rearrange("(a n) -> a n", a=1)).then_inc(bg_loaded, 16)
            sp.wait_ge(x_loaded, 16)
            load(1)
            sp.dma_start(wst[0], Wih.rearrange("p (c j) i -> j (p c) i", j=P)).then_inc(lstm_w_loaded, 16)
            sp.dma_start(wst[1], Whh.rearrange("p (c j) i -> j (p c) i", j=P)).then_inc(lstm_w_loaded, 16)
            with sp.Fori(2, EARLY) as g:
                sp.wait_ge(x_loaded, g * 16)
                load(g)
            sp.wait_ge(wT_done, 2 * MAX_SKIP)
            with sp.Fori(EARLY, GROUPS) as g:
                sp.wait_ge(x_loaded, g * 16)
                load(g)
            with sp.Fori(0, GROUPS) as g:
                sp.wait_ge(out_ready, g + 1)
                sp.dma_start(out[ds(g * GB, GB), :, :].rearrange("b n d -> n b d"),
                             X[:, ds(g * GB, GB), :]).then_inc(out_stored, 16)
            sp.wait_ge(out_stored, 16 * GROUPS)

        @block.gpsimd
        def _(pool):
            g_ = nc.gpsimd
            g_.memset(minus_half[:], -0.5)
            g_.memset(eps[:], LN_EPS)
            g_.memset(ident[:], 0.0)
            g_.memset(v_sb[:, :, :, :, HD:HD + 1], 1.0).then_inc(pool_chain, 1)
            pool.wait_ge(pool_chain, 1)
            g_.affine_select(out=ident[:], in_=ident[:], compare_op=ALU.not_equal, fill=1.0, base=0,
                             pattern=[[-1, P]], channel_multiplier=1).then_inc(pool_chain, 1)
            pool.wait_ge(pool_chain, 2)
            g_.tensor_copy(ident_bf[:], ident[:]).then_inc(consts, 1)

            def rsqrt(layer, g, var, ve, done):
                pool.wait_ge(var, g + 1)
                g_.tensor_tensor(veps[:, layer, :], mv[:, layer, :, 1], eps[:], ALU.add).then_inc(ve, 1)
                pool.wait_ge(ve, g + 1)
                g_.tensor_tensor(rstd[:, layer, :], veps[:, layer, :], minus_half[:], ALU.pow).then_inc(done, 1)

            rsqrt(0, 0, var1, veps1, rstd1)
            rsqrt(0, 1, var1, veps1, rstd1)

            def iteration(s):
                if s.next2:
                    rsqrt(0, s.k + 2, var1, veps1, rstd1)
                if s.mid:
                    rsqrt(1, s.k - 1, var2, veps2, rstd2)

            pipeline(pool, iteration)

            done = 0
            for p, cb, rounds, first in STAGES:
                n_cols = width(p, cb)
                if p == 1:
                    continue
                with pool.Fori(0, rounds) as r:
                    for t in range(1, p):
                        for c in range(SIDE):
                            n = r * (SIDE * p) + (first + t * SIDE + c)
                            pool.wait_ge(gate_acts, n * 4 + (8 + 2))
                            pool.wait_ge(cells, n + 1)
                            g_.tensor_tensor(ig[:, c % 2, 0:n_cols], sig_i[:, c % 2, 0:n_cols],
                                             tanh_g[:, c % 2, 0:n_cols], ALU.mult).then_inc(ig_ready, 1)

        @block.scalar
        def _(act):
            a_ = nc.scalar
            act.dma_start(wqkv[:], W_qkv).then_inc(w_loaded, 16)
            act.dma_start(bias_rows[0:C, :], bih.rearrange("p (c j) -> (p c) j", j=P)).then_inc(w_loaded, 16)
            act.dma_start(bias_rows[C:2 * C, :], bhh.rearrange("p (c j) -> (p c) j", j=P)).then_inc(w_loaded, 16)
            act.dma_start(wg[:, 0, :], Wg0).then_inc(w_loaded, 16)
            act.dma_start(wg[:, 1, :], Wg1).then_inc(w_loaded, 16)

            def exp(s, half):
                act.wait_ge(shifted, s.k * 2 - 1 + half)
                part = prob[:, 2 * half * GT:2 * (half + 1) * GT]
                a_.activation(part, part, ACT.Exp, scale=SCALE).then_inc(exp_ready, 1)

            def read_probT(s, half):
                act.wait_ge(probT_done, s.k * 2 - 1 + half)
                a_.activation(probT[:, 2 * half:2 * half + 2, :], psS[:, 2 * half:2 * half + 2, :], ACT.Copy)\
                    .then_inc(probT_ready, 1)

            act.wait_ge(xnT_done, 1)
            a_.activation(hT[:], psA, ACT.Relu).then_inc(hT_ready, 1)

            def iteration(s):
                k = s.k
                if s.front:
                    act.wait_ge(q_done, k + 1)
                    a_.activation(qT[:], psQ, ACT.Copy).then_inc(q_ready, 1)
                    act.wait_ge(v_done, k + 1)
                    if s.back:
                        act.wait_ge(att_done, k - 1)
                    a_.activation(v_sb[:, s.par, :, :, 0:HD], psA.rearrange("p (b h d) -> p b h d", b=GB, h=HEADS),
                                  ACT.Copy).then_inc(v_ready, 1)
                if s.mid:
                    exp(s, 0)
                if s.front:
                    act.wait_ge(k_done, k + 1)
                    a_.activation(kT[:], psK, ACT.Copy).then_inc(k_ready, 1)
                if s.back:
                    act.wait_ge(xn2T_done, k - 1)
                    a_.activation(h2T[:], psB, ACT.Relu).then_inc(h2T_ready, 1)
                if s.next1:
                    act.wait_ge(xnT_done, k + 2)
                    a_.activation(hT[:], psA, ACT.Relu).then_inc(hT_ready, 1)
                if s.prep:
                    for m in range(2 * MAX_SKIP):
                        act.wait_ge(wT_done, m + 1)
                        a_.activation(W_hi[:, m // MAX_SKIP, m % MAX_SKIP, :], ps[:, 5 + 2 * (m % 2), :], ACT.Copy)\
                            .then_inc(w_hi_done, 1)
                if s.mid:
                    read_probT(s, 0)
                    exp(s, 1)
                if s.back:
                    act.wait_ge(y1_done, k - 1)
                    a_.activation(y_flat, psB, ACT.Copy).then_inc(y1_ready, 1)
                    act.wait_ge(z1_done, k - 1)
                    a_.activation(h1T[:], psA, ACT.Relu).then_inc(h1T_ready, 1)
                if s.mid:
                    read_probT(s, 1)
                if s.back:
                    act.wait_ge(y2_done, k - 1)
                    a_.activation(y_flat, psB, ACT.Copy).then_inc(y2_ready, 1)
                    act.wait_ge(z2_done, k - 1)
                    a_.activation(H_hi[:, ds(k * GT - 2 * GT, GT)], psA, ACT.Relu).then_inc(H_hi_ready, 1)

            pipeline(act, iteration)

            act.wait_ge(H_ready, GROUPS)
            act.wait_ge(att_read, GROUPS)
            act.wait_ge(x2_ready, GROUPS)
            a_.activation(sig_i[:, 0, 0:1], bias[:, 0:1], ACT.Sigmoid).then_inc(gate_acts, 8)

            for p, cb, rounds, first in STAGES:
                n_cols = width(p, cb)
                with act.Fori(0, rounds) as r:
                    def gates(t, c):
                        n = r * (SIDE * p) + (first + t * SIDE + c)
                        for j, (gate, func, to) in enumerate((
                                (0, ACT.Sigmoid, sig_i[:, c % 2, 0:n_cols]), (2, ACT.Tanh, tanh_g[:, c % 2, 0:n_cols]),
                                (1, ACT.Sigmoid, sig_f[:, c % 2, 0:n_cols]), (3, ACT.Sigmoid, sig_o[:, c, 0:n_cols]))):
                            if t == 0 and gate == 1:
                                continue
                            if j == 0:
                                act.wait_ge(cells, n + 1)
                            if j == 3:
                                act.wait_ge(h_f_ready, n + 1)
                            act.wait_ge(gate_sums, n * 4 + (j + 1))
                            a_.activation(to, ps[:, 4 * (c % 2) + j, 0:n_cols], func,
                                          bias=bias[:, GATES * (p - 1) + gate:GATES * (p - 1) + gate + 1])\
                                .then_inc(gate_acts, 2 if t == 0 and j == 1 else 1)

                    def tanh(t, c):
                        n = r * (SIDE * p) + (first + t * SIDE + c)
                        act.wait_ge(cells, n + (2 + 1))
                        act.wait_ge(h_f_ready, n + 3)
                        a_.activation(tanh_c[:, c % 2, 0:n_cols], cell[:, c, 0:n_cols], ACT.Tanh).then_inc(tanhs, 1)

                    order = [(t, c) for t in range(p) for c in range(SIDE)]
                    for m, item in enumerate(order):
                        gates(*item)
                        if m:
                            tanh(*order[m - 1])
                    tanh(*order[-1])

        @block.tensor
        def _(pe):
            mm = nc.tensor.matmul

            def transposed(to, src, n=GB):
                for b in range(n):
                    last = nc.tensor.transpose(to[:, b * P:(b + 1) * P], src[:, b, :], ident[:])
                return last

            pe.wait_ge(consts, 1)
            pe.wait_ge(w_loaded, 16 * 6)
            nc.tensor.transpose(ps[:, 0, 0:P], adj_sb[:], ident[:])
            nc.tensor.transpose(ps[:, 0, P:P + 2 * C], bias_rows[:], ident[0:2 * C, 0:2 * C]).then_inc(adjT_done, 1)

            def graph_linear(layer, hT_in):
                bias_of = lambda part: part[:, layer, :, :].rearrange("a b d -> a (b d)")
                mm(psB, ones_row[:], bias_of(bg_hi), start=True, stop=False)
                mm(psB, ones_row[:], bias_of(bg_lo), start=False, stop=False)
                for b in range(GB):
                    l = mm(psB[:, b * D:(b + 1) * D], hT_in[:, b * N:(b + 1) * N], wg[:, layer, :],
                           start=False, stop=b == GB - 1)
                return l

            def graph_mix():
                for b in range(GB):
                    l = mm(psA[:, b * N:(b + 1) * N], y_sb[:, b, :], adjT[:], start=True, stop=True)
                return l

            def transpose_prob(s, half):
                pe.wait_ge(exp_ready, s.k * 2 - 1 + half)
                pv = prob.rearrange("p (h b n) -> p h b n", h=HEADS, b=GB)
                for h in (2 * half, 2 * half + 1):
                    l = transposed(psS[:, h, :], pv[:, h, :, :])
                l.then_inc(probT_done, 1)

            def attend(s, half):
                pe.wait_ge(probT_ready, s.k * 2 - 1 + half)
                for b in range(GB):
                    for h in (2 * half, 2 * half + 1):
                        o = (b % 2) * HEADS + h
                        l = mm(psO[:, b // 2, o * (HD + 1):(o + 1) * (HD + 1)], probT[:, h, b * N:(b + 1) * N],
                               v_sb[:, 1 - s.par, b, h, :], start=True, stop=True)
                return l

            def put_mask(heads):
                for h in heads:
                    mm(psS[:, h, :].rearrange("p (b n) -> p b n", n=N), ident_bf[:],
                       mask[:].unsqueeze(1).to_broadcast([P, GB, N]), start=True, stop=False)

            pe.wait_ge(xn_ready, 1)
            transposed(psA, xn).then_inc(xnT_done, 1)

            def iteration(s):
                k = s.k
                if s.front:
                    pe.wait_ge(hT_ready, k + 1)
                    if s.back:
                        pe.wait_ge(att_read, k - 1)
                    mm(psQ, wqkv[:, 0:D], hT[:], start=True, stop=True).then_inc(q_done, 1)
                    if s.at > 2:
                        pe.wait_ge(H_ready, k - 2)
                    for b in range(GB):
                        l = mm(psA[:, b * D:(b + 1) * D], hT[:, b * N:(b + 1) * N], wqkv[:, 2 * D:3 * D],
                               start=True, stop=True)
                    l.then_inc(v_done, 1)
                    mm(psK, wqkv[:, D:2 * D], hT[:], start=True, stop=True).then_inc(k_done, 1)
                if s.back:
                    pe.wait_ge(xn2_ready, k - 1)
                    transposed(psB, xn2).then_inc(xn2T_done, 1)
                if s.next1:
                    pe.wait_ge(xn_ready, k + 2)
                    pe.wait_ge(v_ready, k + 1)
                    transposed(psA, xn).then_inc(xnT_done, 1)
                if s.prep:
                    pe.wait_ge(lstm_w_loaded, 32)
                    pe.wait_ge(k_ready, k + 1)
                    for m in range(2 * MAX_SKIP):
                        if m >= 2:
                            pe.wait_ge(w_lo_done, m - 1)
                        w = wst[m // MAX_SKIP][:, GATES * (m % MAX_SKIP):GATES * (m % MAX_SKIP + 1), :]
                        transposed(ps[:, 5 + 2 * (m % 2), :], w).then_inc(wT_done, 1)
                if s.mid:
                    transpose_prob(s, 0)
                if s.back:
                    pe.wait_ge(h2T_ready, k - 1)
                    if s.at == 2:
                        pe.wait_ge(bg_ready, 1)
                    graph_linear(0, h2T).then_inc(y1_done, 1)
                if s.mid:
                    if s.front:
                        pe.wait_ge(k_ready, k + 1)
                        pe.wait_ge(v_ready, k + 1)
                    if s.prep:
                        pe.wait_ge(w_lo_done, 2 * MAX_SKIP)
                    attend(s, 0)
                if s.back:
                    pe.wait_ge(y1_ready, k - 1)
                    if s.next1:
                        pe.wait_ge(hT_ready, k + 2)
                    elif not s.front:
                        pe.wait_ge(H_ready, k - 2)
                    graph_mix().then_inc(z1_done, 1)
                if s.mid:
                    transpose_prob(s, 1)
                if s.back:
                    pe.wait_ge(h1T_ready, k - 1)
                    graph_linear(1, h1T).then_inc(y2_done, 1)
                if s.front:
                    if not s.mid:
                        pe.wait_ge(prep_done, 1)
                    put_mask((0, 1))
                if s.mid:
                    attend(s, 1).then_inc(att_done, 1)
                if s.back:
                    pe.wait_ge(y2_ready, k - 1)
                    graph_mix().then_inc(z2_done, 1)
                if s.front:
                    put_mask((2, 3))
                    pe.wait_ge(k_ready, k + 1)
                    for b in range(GB):
                        for h in range(HEADS):
                            l = mm(psS[:, h, b * N:(b + 1) * N], qT[h * HD:(h + 1) * HD, b * N:(b + 1) * N],
                                   kT[h * HD:(h + 1) * HD, b * N:(b + 1) * N], start=False, stop=b == GB - 1)
                    l.then_inc(scores_done, 1)

            pipeline(pe, iteration)

            for s, (p, cb, rounds, first) in enumerate(STAGES):
                n_cols = width(p, cb)
                if p == 1:
                    pe.wait_ge(H_ready, GROUPS)
                with pe.Fori(0, rounds) as r:
                    for t in range(p):
                        for c in range(SIDE):
                            n = r * (SIDE * p) + (first + t * SIDE + c)
                            chunk = r * SIDE + c
                            if t:
                                pe.wait_ge(steps, n - 3)
                            elif p > 1:
                                p0, cb0, rounds0, first0 = STAGES[s - 1]
                                ratio = cb // cb0
                                lastc = ratio * c + ratio - 1
                                whole, part = lastc // SIDE, lastc % SIDE
                                pe.wait_ge(steps, r * (ratio * SIDE * p0)
                                           + (first0 + whole * SIDE * p0 + (p0 - 1) * SIDE + part + 1))
                            x_hi, x_lo = tokens(H_hi, chunk, p, cb, t), tokens(H_lo, chunk, p, cb, t)
                            for j, gate in enumerate((0, 2, 1, 3)):
                                if t == 0 and gate == 1:
                                    continue
                                pe.wait_ge(gate_acts, n * 4 + (j + 1))
                                to = ps[:, 4 * (c % 2) + j, 0:n_cols]
                                to3 = to.rearrange("k (b w) -> k b w", b=cb)
                                wi = slice(gate * P, (gate + 1) * P)
                                terms = [(to3, W_hi[:, 0, p - 1, wi], x_hi), (to3, W_hi[:, 0, p - 1, wi], x_lo),
                                         (to3, W_lo[:, 0, p - 1, wi], x_hi)]
                                if t:
                                    s_hi, s_lo = S_hi[:, c, 0:n_cols], S_lo[:, c, 0:n_cols]
                                    terms += [(to, W_hi[:, 1, p - 1, wi], s_hi), (to, W_hi[:, 1, p - 1, wi], s_lo),
                                              (to, W_lo[:, 1, p - 1, wi], s_hi)]
                                for m, (o, w, v) in enumerate(terms):
                                    l = mm(o, w, v, start=m == 0, stop=m == len(terms) - 1)
                                l.then_inc(gate_sums, 2 if t == 0 and j == 1 else 1)

            with pe.Fori(0, GROUPS // 2) as r:
                for u in range(2):
                    pe.wait_ge(h_sum, r * 2 + (u + 1))
                    transposed(ps[:, u, :], h_out[:, u, :].rearrange("p (b n) -> p b n", b=GB)).then_inc(hT_out, 1)

        @block.vector
        def _(dve):
            v_ = nc.vector
            def moments(layer, g, stats_ready, var):
                for b in range(GB):
                    l = v_.bn_stats(stats[:, layer, b, :], X[:, ds(g * GB + b, 1), :].rearrange("p a d -> p (a d)"))
                l.then_inc(stats_ready, 1)
                dve.wait_ge(stats_ready, g + 1)
                v_.memset(pause[:], 0.0)
                for b in range(GB):
                    l = v_.bn_aggr(mv[:, layer, b, :], stats[:, layer, b, :])
                l.then_inc(var, 1)

            def normalize(layer, g, to, rstd_ready, ready):
                dve.wait_ge(rstd_ready, g + 1)
                for b in range(GB):
                    l = v_.tensor_scalar(to[:, b, :], X[:, ds(g * GB + b, 1), :].rearrange("p a d -> p (a d)"),
                                         mv[:, layer, b, 0:1], rstd[:, layer, b:b + 1], ALU.subtract, ALU.mult)
                l.then_inc(ready, 1)

            dve.wait_ge(x_loaded, 16)
            moments(0, 0, stats1, var1)
            normalize(0, 0, xn, rstd1, xn_ready)
            dve.wait_ge(x_loaded, 32)
            moments(0, 1, stats1, var1)
            dve.wait_ge(xnT_done, 1)
            normalize(0, 1, xn, rstd1, xn_ready)
            v_.memset(ones_f[:], 1.0).then_inc(bg_copied, 1)
            dve.wait_ge(adjT_done, 1)
            v_.tensor_scalar(mask[:], adj_sb[:], 0.0, MASKED, ALU.is_equal, ALU.mult)
            v_.tensor_copy(adjT[:], ps[:, 0, 0:P])
            v_.tensor_copy(bias_2[:], ps[:, 0, P:P + 2 * C]).then_inc(prep_done, 1)
            dve.wait_ge(prep_done, 1)
            v_.tensor_tensor(bias[:], bias_2[:, 0:C], bias_2[:, C:2 * C], ALU.add)
            dve.wait_ge(bg_loaded, 32)
            v_.tensor_copy(bg_f[:], bg_rows[:].unsqueeze(2).to_broadcast([1, 2, GB, D])).then_inc(bg_copied, 1)
            dve.wait_ge(bg_copied, 2)
            v_.tensor_copy(ones_row[:], ones_f[:])
            v_.tensor_copy(bg_hi[:], bg_f[:]).then_inc(bg_hi_ready, 1)
            dve.wait_ge(bg_hi_ready, 1)
            v_.tensor_tensor(bg_lo[:], bg_f[:], bg_hi[:].bitcast(F32), ALU.subtract).then_inc(bg_ready, 1)

            s3 = psS.rearrange("p h (b n) -> p (h b) n", n=N)
            o4 = psO[:, :, 0:2 * HEADS * (HD + 1)].rearrange("p a (c d) -> p a c d", d=HD + 1)
            r3 = rec[:].rearrange("p (a c) -> p a c", a=2)

            def shift(s, half):
                part = slice(2 * half * GB, 2 * (half + 1) * GB)
                v_.tensor_reduce(rmax[:, part], s3[:, part, :], AX_X, ALU.max).then_inc(max_ready, 1)
                dve.wait_ge(max_ready, s.k * 2 - 1 + half)
                v_.tensor_tensor(prob.rearrange("p (c n) -> p c n", n=N)[:, part, :], s3[:, part, :],
                                 rmax[:, part].unsqueeze(2).to_broadcast([P, 2 * GB, N]), ALU.subtract)\
                    .then_inc(shifted, 1)

            def iteration(s):
                k = s.k
                if s.mid:
                    dve.wait_ge(scores_done, k)
                    shift(s, 0)
                    shift(s, 1)
                if s.prep:
                    for m in range(2 * MAX_SKIP):
                        dve.wait_ge(w_hi_done, m + 1)
                        v_.tensor_tensor(W_lo[:, m // MAX_SKIP, m % MAX_SKIP, :], ps[:, 5 + 2 * (m % 2), :],
                                         W_hi[:, m // MAX_SKIP, m % MAX_SKIP, :].bitcast(F32), ALU.subtract)\
                            .then_inc(w_lo_done, 1)
                if s.next2:
                    dve.wait_ge(x_loaded, k * 16 + 48)
                    moments(0, k + 2, stats1, var1)
                    dve.wait_ge(xnT_done, k + 2)
                    normalize(0, k + 2, xn, rstd1, xn_ready)
                if s.mid:
                    dve.wait_ge(att_done, k)
                    v_.reciprocal(r3, o4[:, :, :, HD]).then_inc(rec_ready, 1)
                    dve.wait_ge(rec_ready, k)
                    v_.tensor_tensor(att.rearrange("p (a c d) -> p a c d", a=2, d=HD), o4[:, :, :, 0:HD],
                                     r3.unsqueeze(3).to_broadcast([P, 2, 2 * HEADS, HD]), ALU.mult).then_inc(att_read, 1)
                    dve.wait_ge(att_read, k)
                    xg = X[:, ds(k * GB - GB, GB), :]
                    v_.tensor_tensor(xg, xg, att.rearrange("p (b d) -> p b d", b=GB), ALU.add).then_inc(x2_ready, 1)
                    dve.wait_ge(x2_ready, k)
                    moments(1, k - 1, stats2, var2)
                if s.back:
                    dve.wait_ge(H_hi_ready, k - 1)
                    at_ = ds(k * GT - 2 * GT, GT)
                    v_.scalar_tensor_tensor(H_lo[:, at_], psA, 0.0, H_hi[:, at_].bitcast(F32),
                                            ALU.max, ALU.subtract).then_inc(H_ready, 1)
                if s.mid:
                    normalize(1, k - 1, xn2, rstd2, xn2_ready)

            pipeline(dve, iteration)

            dve.wait_ge(gate_acts, 8)
            v_.memset(released[:, 0:1], 0.0).then_inc(cells, 2)
            v_.memset(released[:, 1:2], 0.0).then_inc(h_f_ready, 4)
            later = 0
            for p, cb, rounds, first in STAGES:
                n_cols = width(p, cb)
                with dve.Fori(0, rounds) as r:
                    def cell_part(t, c):
                        n = r * (SIDE * p) + (first + t * SIDE + c)
                        dve.wait_ge(gate_acts, n * 4 + (8 + 2 if t == 0 else 8 + 3))
                        if t == 0:
                            v_.tensor_tensor(cell[:, c, 0:n_cols], sig_i[:, c % 2, 0:n_cols],
                                             tanh_g[:, c % 2, 0:n_cols], ALU.mult).then_inc(cells, 1)
                            return
                        m = r * (SIDE * (p - 1)) + (later + (t - 1) * SIDE + c + 1)
                        v_.tensor_tensor(cell[:, c, 0:n_cols], sig_f[:, c % 2, 0:n_cols],
                                         cell[:, c, 0:n_cols], ALU.mult).then_inc(fc_ready, 1)
                        dve.wait_ge(fc_ready, m)
                        dve.wait_ge(ig_ready, m)
                        v_.tensor_tensor(cell[:, c, 0:n_cols], cell[:, c, 0:n_cols],
                                         ig[:, c % 2, 0:n_cols], ALU.add).then_inc(cells, 1)

                    def state_part(t, c):
                        n = r * (SIDE * p) + (first + t * SIDE + c)
                        chunk = r * SIDE + c
                        dve.wait_ge(gate_acts, n * 4 + (8 + 4))
                        dve.wait_ge(tanhs, n + 1)
                        if t == p - 1:
                            hi, lo = tokens(H_hi, chunk, p, cb, t), tokens(H_lo, chunk, p, cb, t)
                        else:
                            hi, lo = S_hi[:, c, 0:n_cols], S_lo[:, c, 0:n_cols]
                        h = h_f[:, c % 2, 0:n_cols]
                        v_.tensor_tensor(h, sig_o[:, c, 0:n_cols], tanh_c[:, c % 2, 0:n_cols], ALU.mult)\
                            .then_inc(h_f_ready, 1)
                        if t == p - 1:
                            h = h.rearrange("k (b w) -> k b w", b=cb)
                        dve.wait_ge(h_f_ready, n + (4 + 1))
                        v_.tensor_copy(hi, h).then_inc(s_hi_ready, 1)
                        dve.wait_ge(s_hi_ready, n + 1)
                        v_.tensor_tensor(lo, h, hi.bitcast(F32), ALU.subtract).then_inc(steps, 1)

                    order = [(t, c) for t in range(p) for c in range(SIDE)]
                    for m, item in enumerate(order):
                        cell_part(*item)
                        if m:
                            state_part(*order[m - 1])
                    state_part(*order[-1])
                later += rounds * SIDE * (p - 1)

            dve.wait_ge(steps, ITEMS)

            def h_whole(g, u):
                v_.tensor_tensor(h_out[:, u, :], H_hi[:, ds(g * GT, GT)].bitcast(F32),
                                 H_lo[:, ds(g * GT, GT)].bitcast(F32), ALU.add).then_inc(h_sum, 1)

            with dve.Fori(0, GROUPS // 2) as r:
                for u in range(2):
                    h_whole(r * 2 + u, u)
                for u in range(2):
                    g = r * 2 + u
                    dve.wait_ge(hT_out, g + 1)
                    xg = X[:, ds(g * GB, GB), :]
                    v_.tensor_tensor(xg, xg, ps[:, u, :].rearrange("p (b d) -> p b d", b=GB), ALU.add)\
                        .then_inc(out_ready, 1)


_INS = ['x', 'adj', 'L0_gnn_W', 'L1_gnn_Wg0', 'L1_gnn_bg0', 'L1_gnn_Wg1', 'L1_gnn_bg1', 'L1_gnn_Wih', 'L1_gnn_Whh',
        'L1_gnn_bih', 'L1_gnn_bhh']


def kernel(**inputs):
    import numpy as _np
    import concourse.bacc as _bacc
    from concourse import mybir as _mybir
    from concourse.bass_utils import run_bass_kernel_spmd as _run

    nc = _bacc.Bacc("TRN2", target_bir_lowering=False, num_devices=1)
    arrays, args = {}, []
    for name in _INS:
        a = _np.ascontiguousarray(inputs[name])
        arrays[f"in_{name}_dram"] = a
        args.append(nc.dram_tensor(f"in_{name}_dram", a.shape, _mybir.dt.from_np(a.dtype), kind="ExternalInput").ap())
    shape = inputs['x'].shape
    args.append(nc.dram_tensor("out_0_dram", shape, _mybir.dt.float32, kind="ExternalOutput").ap())
    gnn_block(nc, *args)
    r = _run(nc, [arrays], core_ids=[0])
    return r.results[0]["out_0_dram"]
```

```python
from contextlib import ExitStack

import concourse.bass as bass
from concourse import mybir

F32 = mybir.dt.float32
F32R = mybir.dt.float32r
BF16 = mybir.dt.bfloat16
ALU = mybir.AluOpType
ACT = mybir.ActivationFunctionType
AX_X = mybir.AxisListType.X
ds = bass.ds

LN_EPS = 1e-5
MASKED = -1e30
BANK = 512
MAX_SKIP = 4


def gnn_block(
    nc: bass.Bass,
    x: bass.AP,
    adj: bass.AP,
    W_qkv: bass.AP,
    Wg0: bass.AP,
    bg0: bass.AP,
    Wg1: bass.AP,
    bg1: bass.AP,
    Wih: bass.AP,
    Whh: bass.AP,
    bih: bass.AP,
    bhh: bass.AP,
    out: bass.AP,
):
    B, N, D = x.shape
    P = 128
    assert N == P and D == P
    HEADS = 4
    HD = D // HEADS
    SCALE = float(HD) ** -0.5
    GB = BANK // N
    GROUPS = B // GB
    GT = GB * N
    GATES = 4

    OUT = "out"
    BATCHES = {1: 4, 2: 8, 3: 8, 4: 16}
    CHUNKS = {p: B // cb for p, cb in BATCHES.items()}
    LOOPED = {2: 2, 3: 2, 4: 0}
    SLOTS = {1: 3, 2: 4, 3: 6, 4: 4}

    def slots_of(p, t, chunk):
        if p == 1:
            return 2, 2
        if p in (2, 3):
            return 2 * t + (t + chunk) % 2, 2 * (t - 1) + (t - 1 + chunk) % 2
        return chunk % SLOTS[p], chunk % SLOTS[p]

    def width(p):
        return BATCHES[p] * (N // p)

    class Item:
        def __init__(self, p, t, chunk, n, par, buf, slots, later, steps, needs, ahead, waits):
            self.needs, self.ahead = needs, ahead
            self.waits = waits
            self.p, self.t, self.chunk, self.n = p, t, chunk, n
            self.par = par
            self.buf = buf
            self.slots = slots
            self.later, self.steps = later, steps

        def moved(self, rounds, items):
            later = sum(1 for i in items if i.t != 0)
            return Item(self.p, self.t, self.chunk + rounds * 2, self.n + rounds * len(items),
                        self.par, self.buf, self.slots, self.later + rounds * later, self.steps + rounds * len(items),
                        self.needs + rounds * self.ahead, self.ahead, self.waits)

    segments = []
    number = later_steps = steps_before = 0
    done_at = {}

    def made(p, t, chunk):
        nonlocal number, later_steps, steps_before
        if t == OUT:
            needs = 0
        elif t:
            needs = done_at[p, t - 1, chunk]
        elif p > 1:
            ratio = BATCHES[p] // BATCHES[p - 1]
            if p == 2:
                needs = done_at.get((1, 0, CHUNKS[1] - 1), 0) if chunk % 2 == (CHUNKS[2] - 1) % 2 else 0
            else:
                needs = done_at[p - 1, p - 2, ratio * chunk + ratio - 1]
        else:
            needs = 0
        it = Item(p, t, chunk, number, number % 2 if number >= AHEAD else 0, steps_before % 2,
                  t != OUT and slots_of(p, t, chunk), later_steps, steps_before, needs, 0, needs > 0)
        if t != OUT:
            done_at[p, t, chunk] = steps_before + 1
        number += 1
        later_steps += t not in (0, OUT)
        steps_before += t != OUT
        return it

    def straight(p, t, chunk):
        segments.append((1, [made(p, t, chunk)]))

    AHEAD = 3
    for p in range(2, MAX_SKIP + 1):
        d, last_diagonal = 0, CHUNKS[p] + p - 2
        while d <= last_diagonal:
            if LOOPED[p] and d == CHUNKS[p] - 2 * LOOPED[p]:
                here = [(t, d + e - t) for e in range(2) for t in range(p)]
                assert len(here) % 2 == 0
                rounds = [[made(p, t, c + 2 * r) for t, c in here] for r in range(LOOPED[p])]
                for m, it in enumerate(rounds[0]):
                    it.ahead = rounds[1][m].needs - it.needs
                    assert all(it.needs + r * it.ahead >= rounds[r][m].needs for r in range(LOOPED[p]))
                    assert all(it.needs + r * it.ahead < rounds[r][m].steps for r in range(LOOPED[p]))
                segments.append((LOOPED[p], rounds[0]))
                d += 2 * LOOPED[p]
                continue
            for t in range(p):
                if d == last_diagonal and p < MAX_SKIP:
                    break
                if 0 <= d - t < CHUNKS[p]:
                    straight(p, t, d - t)
                    if d == 0 and p > 2:
                        straight(p - 1, p - 2, CHUNKS[p - 1] - 1)
                    if number == AHEAD + 1:
                        straight(1, 0, CHUNKS[1] - 1)
            if p == MAX_SKIP and CHUNKS[p] <= d < last_diagonal:
                straight(p, OUT, d - CHUNKS[p])
            d += 1
    for chunk in range(CHUNKS[MAX_SKIP] - 2, CHUNKS[MAX_SKIP]):
        straight(MAX_SKIP, OUT, chunk)

    early = [items[0] for rounds, items in segments[:AHEAD]]
    assert all(rounds == 1 for rounds, items in segments[:AHEAD])

    def banks_free(it, j):
        return it.n * 4 + (j + 1 if it in early else j - 3)

    def gates_read(it, j):
        return it.n * 4 + (4 + j)

    def is_last(it):
        return it.p == MAX_SKIP and it.t == it.p - 1 and it.chunk == CHUNKS[MAX_SKIP] - 1

    def walk(eng, visit):
        prev = early[-1]
        for rounds, items in segments[AHEAD:]:
            if rounds == 1:
                for it in items:
                    visit(it, prev)
                    prev = it
                continue
            assert prev.p == items[-1].p and prev.t == items[-1].t and prev.n + 1 == items[0].n
            with eng.Fori(0, rounds) as r:
                back = items[-1].moved(-1, items).moved(r, items)
                for it in items:
                    it = it.moved(r, items)
                    visit(it, back)
                    back = it
            prev = items[-1].moved(rounds - 1, items)
        visit(None, prev)

    with ExitStack() as ctx:
        def sb(name, shape, dt=F32):
            return ctx.enter_context(nc.sbuf_tensor(name, shape, dt))

        def sem(name):
            return ctx.enter_context(nc.semaphore(name))

        X = sb("X", [P, B, D])
        H_hi = sb("H_hi", [P, B * N], F32R)
        H_lo = sb("H_lo", [P, B * N], F32R)
        W_hi = sb("W_hi", [P, 2, MAX_SKIP, GATES * P], F32R)
        W_lo = sb("W_lo", [P, 2, MAX_SKIP, GATES * P], F32R)
        ident = sb("ident", [P, P])
        ident_bf = sb("ident_bf", [P, P], BF16)
        mask = sb("mask", [P, N], BF16)
        adj_sb = sb("adj_sb", [P, N])
        adjT = sb("adjT", [P, N])
        wv = sb("wv", [P, D])
        wqk_hi = sb("wqk_hi", [P, 2 * D], F32R)
        wqk_lo = sb("wqk_lo", [P, 2 * D], F32R)
        wg = sb("wg", [P, 2, D])
        PART = 32
        ROWS = 3 * PART
        bg_rows = sb("bg_rows", [ROWS, 2, D])
        bg_parts = sb("bg_parts", [ROWS, 2, D], F32R)
        sums_parts = sb("sums_parts", [ROWS, N], F32R)
        ones_f = sb("ones_f", [P, ROWS])
        bias_rows = sb("bias_rows", [2 * MAX_SKIP * GATES, P])
        bias_2 = sb("bias_2", [P, 2 * MAX_SKIP * GATES])
        bias = sb("bias", [P, MAX_SKIP * GATES])
        half_bias = sb("half_bias", [P, GATES])
        stats = sb("stats", [P, 2, GB, 6])
        mv = sb("mv", [P, 2, GB, 2])
        veps = sb("veps", [P, 2, GB])
        rstd = sb("rstd", [P, 2, GB])
        minus_half = sb("minus_half", [P, GB])
        eps = sb("eps", [P, GB])
        pause = sb("pause", [P, 1])
        released = sb("released", [P, 2])
        rmax = sb("rmax", [P, HEADS * GB])
        rec = sb("rec", [P, GB * HEADS])
        STATE = max(SLOTS[p] * width(p) for p in range(1, MAX_SKIP + 1))
        S_hi = sb("S_hi", [P, STATE], F32R)
        S_lo = sb("S_lo", [P, STATE], F32R)

        V = 2 * GB * HEADS * (HD + 1)
        ARENA = 23 * GT
        arena = sb("arena", [P, ARENA])
        at = [0]

        def take(n):
            v = arena[:, at[0]:at[0] + n]
            at[0] += n
            return v

        tokens_first = lambda: take(GT).rearrange("p (b d) -> p b d", b=GB)
        xn = tokens_first()
        hT = take(GT)
        hT_hi = S_hi[:, 0:2 * GT].rearrange("p (s n) -> p s n", s=2)
        hT_lo = S_lo[:, 0:2 * GT].rearrange("p (s n) -> p s n", s=2)
        qT, kT, att = take(GT), take(GT), take(GT)
        v_sb = take(V).rearrange("p (s b h d) -> p s b h d", s=2, b=GB, h=HEADS)
        prob = take(HEADS * GT)
        wqk_raw = prob[:, 0:2 * D]
        probT = take(HEADS * GT).rearrange("p (h n) -> p h n", h=HEADS)
        at[0] = attention_end = 16 * GT
        xn2 = tokens_first()
        hn2 = xn2.rearrange("p b d -> p (b d)")
        h1, u2T = take(GT), take(GT)
        act_i, act_g, act_o, u1T = take(GT), take(GT), take(GT), take(GT)
        assert at[0] == ARENA
        C = MAX_SKIP * GATES
        wst = [X[:, B - 2 * C:B - C, :], X[:, B - C:B, :]]
        EARLY = (B - 2 * C) // GB
        at[0] = 0
        pair = lambda: take(2 * BANK).rearrange("p (s n) -> p s n", s=2)
        sig_i, tanh_g, sig_f, sig_o, ig, tanh_c, h_f = (pair() for _ in range(7))
        assert at[0] + 2 * width(2) == attention_end
        cell = take(STATE)
        spare = take(GT)
        assert at[0] <= ARENA - 4 * BANK
        at[0] = ARENA - 4 * BANK
        h_out = take(4 * BANK).rearrange("p (s n) -> p s n", s=4)

        def finished(chunk, j):
            if chunk < CHUNKS[MAX_SKIP] - 1:
                return h_out[:, j, :]
            return cell[:, j * GT:(j + 1) * GT] if j < OUT_GROUPS - 1 else spare

        ps = ctx.enter_context(nc.psum_tensor("ps", [P, 8, BANK], F32))
        psS = ps[:, 0:HEADS, :]
        psA = ps[:, 6, :]
        psB = ps[:, 7, :]
        psQ = ps[:, 4, :]
        psK = ps[:, 5, :]
        psX = {True: psK, False: psB}
        psO = ps[:, 4:6, :]

        def psW(m):
            return ps[:, m, :] if m < MAX_SKIP else (psA, psQ, psB, psA)[m - MAX_SKIP]

        x_loaded = sem("x_loaded")
        w_loaded = sem("w_loaded")
        wg_loaded = sem("wg_loaded")
        wih_loaded = sem("wih_loaded")
        whh_loaded = sem("whh_loaded")
        bg_loaded = sem("bg_loaded")
        ones_set = sem("ones_set")
        bg_zeroed = sem("bg_zeroed")
        sums_done = sem("sums_done")
        sums_hi = sem("sums_hi")
        sums_ready = sem("sums_ready")
        parts_hi = sem("parts_hi")
        bg_ready = sem("bg_ready")
        consts = sem("consts")
        pool_chain = sem("pool_chain")
        wT_done = sem("wT_done")
        w_hi_done = sem("w_hi_done")
        w_lo_done = sem("w_lo_done")
        adjT_done = sem("adjT_done")
        prep_done = sem("prep_done")
        bias_ready = sem("bias_ready")
        var1 = sem("var1")
        rstd1 = sem("rstd1")
        var2 = sem("var2")
        rstd2 = sem("rstd2")
        veps1 = sem("veps1")
        veps2 = sem("veps2")
        stats1 = sem("stats1")
        stats2 = sem("stats2")
        xn_ready = sem("xn_ready")
        xnT_done = sem("xnT_done")
        hT_ready = sem("hT_ready")
        hT_hi_ready = sem("hT_hi_ready")
        hT_lo_ready = sem("hT_lo_ready")
        wqk_hi_ready = sem("wqk_hi_ready")
        wqk_ready = sem("wqk_ready")
        q_done = sem("q_done")
        q_ready = sem("q_ready")
        k_done = sem("k_done")
        k_ready = sem("k_ready")
        v_done = sem("v_done")
        v_ready = sem("v_ready")
        scores_done = sem("scores_done")
        max_ready = sem("max_ready")
        shifted = sem("shifted")
        exp_ready = sem("exp_ready")
        probT_done = sem("probT_done")
        probT_ready = sem("probT_ready")
        att_done = sem("att_done")
        rec_ready = sem("rec_ready")
        att_read = sem("att_read")
        x2_ready = sem("x2_ready")
        xn2_ready = sem("xn2_ready")
        hn2_ready = sem("hn2_ready")
        u1_done = sem("u1_done")
        u1T_ready = sem("u1T_ready")
        z1_done = sem("z1_done")
        h1_ready = sem("h1_ready")
        u2_done = sem("u2_done")
        u2T_ready = sem("u2T_ready")
        z2_done = sem("z2_done")
        H_hi_ready = sem("H_hi_ready")
        H_ready = sem("H_ready")
        first_sums = sem("first_sums")
        first_acts = sem("first_acts")
        first_cell = sem("first_cell")
        first_h = sem("first_h")
        first_hi = sem("first_hi")
        first_done = sem("first_done")
        gate_sums = sem("gate_sums")
        gate_acts = sem("gate_acts")
        ig_ready = sem("ig_ready")
        fc_ready = sem("fc_ready")
        cells = sem("cells")
        tanhs = sem("tanhs")
        h_f_ready = sem("h_f_ready")
        s_hi_ready = sem("s_hi_ready")
        steps = sem("steps")
        h_sum = sem("h_sum")
        most_ready = sem("most_ready")
        x_added = sem("x_added")
        out_ready = sem("out_ready")
        out_stored = sem("out_stored")

        block = ctx.enter_context(nc.Block())

        def tokens(T, it):
            p, size = it.p, BATCHES[it.p] * N
            v = T[:, ds(it.chunk * size, size)].rearrange("k (b n) -> k b n", n=N)
            return v[:, :, 0:N // p * p].rearrange("k b (w q) -> k b w q", q=p)[:, :, :, it.t]

        def slot(T, it, before=0):
            w = width(it.p)
            return T[:, it.slots[before] * w:(it.slots[before] + 1) * w]

        OUT_GROUPS = BATCHES[MAX_SKIP] // GB

        class Step:

            def __init__(self, k, at=None):
                at = k if at is None else at
                self.k, self.par, self.at = k, at % 2, at
                self.front, self.mid, self.back = at < GROUPS, 1 <= at <= GROUPS, 2 <= at
                self.finish, self.after, self.last = 3 <= at, 4 <= at, at == GROUPS + 1
                self.next1, self.next2 = at + 1 < GROUPS, at + 2 < GROUPS
                self.prep = at < 2
                self.weights = range(at * MAX_SKIP, (at + 1) * MAX_SKIP)

        def pipeline(eng, iteration):
            iteration(Step(0))
            iteration(Step(1))
            iteration(Step(2))
            iteration(Step(3))
            with eng.Fori(0, (GROUPS - 6) // 2) as r:
                iteration(Step(r * 2 + 4, 4))
                iteration(Step(r * 2 + 5, 5))
            for k in range(GROUPS - 2, GROUPS + 2):
                iteration(Step(k))

        @block.sync
        def _(sp):
            def load(g):
                sp.dma_start(X[:, ds(g * GB, GB), :],
                             x[ds(g * GB, GB), :, :].rearrange("b n d -> n b d")).then_inc(x_loaded, 16)

            load(0)
            sp.dma_start(adj_sb[:], adj).then_inc(w_loaded, 16)
            sp.wait_ge(x_loaded, 16)
            sp.dma_start(wst[0], Wih.rearrange("p (c j) i -> j (p c) i", j=P)).then_inc(wih_loaded, 16)
            load(1)
            sp.dma_start(wst[1], Whh.rearrange("p (c j) i -> j (p c) i", j=P)).then_inc(whh_loaded, 16)
            sp.wait_ge(bg_zeroed, 1)
            for row in range(0, ROWS, PART):
                sp.dma_start(bg_rows[row:row + 1, 0, :], bg0.rearrange("(a n) -> a n", a=1)).then_inc(bg_loaded, 16)
                sp.dma_start(bg_rows[row:row + 1, 1, :], bg1.rearrange("(a n) -> a n", a=1)).then_inc(bg_loaded, 16)
            with sp.Fori(2, EARLY) as g:
                sp.wait_ge(x_loaded, g * 16)
                load(g)
            sp.wait_ge(wT_done, 2 * MAX_SKIP)
            with sp.Fori(EARLY, GROUPS) as g:
                sp.wait_ge(x_loaded, g * 16)
                load(g)

            def store(g):
                sp.dma_start(out[ds(g * GB, GB), :, :].rearrange("b n d -> n b d"),
                             X[:, ds(g * GB, GB), :]).then_inc(out_stored, 16)

            with sp.Fori(0, GROUPS - OUT_GROUPS) as g:
                sp.wait_ge(x_added, g + 1)
                store(g)
            for j in range(0, OUT_GROUPS, 2):
                sp.wait_ge(out_ready, j + 1)
                store(j + (GROUPS - OUT_GROUPS))
            sp.wait_ge(out_stored, 16 * GROUPS)

        @block.gpsimd
        def _(pool):
            g_ = nc.gpsimd
            g_.memset(minus_half[:], -0.5)
            g_.memset(eps[:], LN_EPS)
            g_.memset(ident[:], 0.0)
            g_.memset(v_sb[:, :, :, :, HD:HD + 1], 1.0).then_inc(pool_chain, 1)
            pool.wait_ge(pool_chain, 1)
            g_.affine_select(out=ident[:], in_=ident[:], compare_op=ALU.not_equal, fill=1.0, base=0,
                             pattern=[[-1, P]], channel_multiplier=1).then_inc(pool_chain, 1)
            pool.wait_ge(pool_chain, 2)
            g_.tensor_copy(ident_bf[:], ident[:]).then_inc(consts, 1)
            g_.memset(bg_rows[:], 0.0).then_inc(bg_zeroed, 1)

            def rsqrt(layer, g, var, ve, done):
                pool.wait_ge(var, g + 1)
                g_.tensor_tensor(veps[:, layer, :], mv[:, layer, :, 1], eps[:], ALU.add).then_inc(ve, 1)
                pool.wait_ge(ve, g + 1)
                g_.tensor_tensor(rstd[:, layer, :], veps[:, layer, :], minus_half[:], ALU.pow).then_inc(done, 1)

            rsqrt(0, 0, var1, veps1, rstd1)
            rsqrt(0, 1, var1, veps1, rstd1)

            def iteration(s):
                if s.next2:
                    rsqrt(0, s.k + 2, var1, veps1, rstd1)
                if s.mid:
                    rsqrt(1, s.k - 1, var2, veps2, rstd2)

            pipeline(pool, iteration)

            def visit(it, prev):
                if it and it.t == OUT and it.chunk < CHUNKS[MAX_SKIP] - 1:
                    for j in range(OUT_GROUPS):
                        g = it.chunk * OUT_GROUPS + j
                        pool.wait_ge(gate_acts, gates_read(it, j + 1))
                        xg = X[:, g * GB:(g + 1) * GB, :]
                        g_.tensor_tensor(xg, xg, h_out[:, j, :].rearrange("p (b d) -> p b d", b=GB), ALU.add)\
                            .then_inc(x_added, 1)
                elif it and it.t != 0 and it.t != OUT:
                    w = width(it.p)
                    pool.wait_ge(gate_acts, gates_read(it, 2))
                    pool.wait_ge(cells, it.steps + 1)
                    g_.tensor_tensor(ig[:, it.buf, 0:w], sig_i[:, it.buf, 0:w], tanh_g[:, it.buf, 0:w], ALU.mult)\
                        .then_inc(ig_ready, 1)

            for m, it in enumerate(early):
                visit(it, early[m - 1] if m else None)
            walk(pool, visit)

        @block.scalar
        def _(act):
            a_ = nc.scalar
            act.dma_start(wqk_raw, W_qkv[:, 0:2 * D]).then_inc(w_loaded, 16)
            act.dma_start(wv[:], W_qkv[:, 2 * D:3 * D]).then_inc(w_loaded, 16)
            act.dma_start(bias_rows[0:C, :], bih.rearrange("p (c j) -> (p c) j", j=P)).then_inc(w_loaded, 16)
            act.dma_start(bias_rows[C:2 * C, :], bhh.rearrange("p (c j) -> (p c) j", j=P)).then_inc(w_loaded, 16)
            act.dma_start(wg[:, 0, :], Wg0).then_inc(wg_loaded, 16)
            act.dma_start(wg[:, 1, :], Wg1).then_inc(wg_loaded, 16)

            def read(to, psum, done, count, ready, func=ACT.Copy):
                act.wait_ge(done, count)
                a_.activation(to, psum, func).then_inc(ready, 1)

            def exp(s, half):
                act.wait_ge(shifted, s.k * 2 - 1 + half)
                part = prob[:, 2 * half * GT:2 * (half + 1) * GT]
                a_.activation(part, part, ACT.Exp, scale=SCALE).then_inc(exp_ready, 1)

            def read_probT(s, half):
                read(probT[:, 2 * half:2 * half + 2, :], psS[:, 2 * half:2 * half + 2, :],
                     probT_done, s.k * 2 - 1 + half, probT_ready)

            def first_gate(g, m, to, gate, scale):
                act.wait_ge(first_sums, g * 3 + (m + 1))
                b = bias if scale == 1.0 else half_bias
                a_.activation(to[:], psB, ACT.Tanh, bias=b[:, gate:gate + 1], scale=scale).then_inc(first_acts, 1)

            def read_output(g):
                read(H_hi[:, ds(g * GT, GT)], psB, z2_done, g + 1, H_hi_ready, ACT.Relu)

            def tanh(it):
                act.wait_ge(cells, it.steps + (2 + 1))
                act.wait_ge(h_f_ready, it.steps + 1)
                a_.activation(tanh_c[:, it.buf, 0:width(it.p)], slot(cell, it), ACT.Tanh).then_inc(tanhs, 1)

            def gates(it, prev):
                w = width(it.p)
                for j, (gate, func, to) in enumerate(((0, ACT.Sigmoid, sig_i), (2, ACT.Tanh, tanh_g),
                                                      (1, ACT.Sigmoid, sig_f), (3, ACT.Sigmoid, sig_o))):
                    if it.t == 0 and gate == 1:
                        continue
                    if j == 0:
                        act.wait_ge(cells, it.steps + 1)
                    if j == 3:
                        act.wait_ge(h_f_ready, it.steps + 1)
                    act.wait_ge(gate_sums, it.n * 4 + (j + 1))
                    col = GATES * (it.p - 1) + gate
                    a_.activation(to[:, it.buf, 0:w], ps[:, 4 * it.par + j, 0:w], func, bias=bias[:, col:col + 1])\
                        .then_inc(gate_acts, 2 if it.t == 0 and j == 1 else 1)
                    if j == 0 and prev and prev.t != OUT:
                        tanh(prev)

            def visit(it, prev):
                if it and it.t != OUT:
                    gates(it, prev)
                    return
                outputs = range(OUT_GROUPS) if it and it.chunk < CHUNKS[MAX_SKIP] - 1 else range(0)
                for j in outputs:
                    if prev.t != OUT and j == (OUT_GROUPS - 1 if is_last(prev) else 0):
                        tanh(prev)
                    act.wait_ge(gate_sums, it.n * 4 + (j + 1))
                    a_.activation(h_out[:, j, :], ps[:, 4 * it.par + j, :], ACT.Copy).then_inc(gate_acts, 1)

            def read_hT(psum, count, par):
                act.wait_ge(xnT_done, count)
                a_.activation(hT, psum, ACT.Relu).then_inc(hT_ready, 1)
                a_.activation(hT_hi[:, par, :], psum, ACT.Relu).then_inc(hT_hi_ready, 1)

            def read_weight(m):
                read(W_hi[:, m // MAX_SKIP, m % MAX_SKIP, :], psW(m), wT_done, m + 1, w_hi_done)

            act.wait_ge(w_loaded, 16 * 5)
            a_.activation(wqk_hi[:], wqk_raw, ACT.Copy).then_inc(wqk_hi_ready, 1)
            read_hT(psB, 1, 0)
            read_weight(0)
            read_weight(1)

            def last_iteration(k):
                read_output(k - 3)
                read(hn2, hn2, xn2_ready, k - 1, hn2_ready, ACT.Relu)
                visit(early[1], early[0])
                read(u1T[:], psA, u1_done, k - 1, u1T_ready)
                act.wait_ge(first_h, k - 3)
                first_gate(k - 3, 0, act_i, 0, 0.5)
                read(h1[:], psA, z1_done, k - 1, h1_ready, ACT.Relu)
                first_gate(k - 3, 1, act_g, 2, 1.0)
                act.wait_ge(first_cell, k - 2)
                a_.activation(act_i[:], act_g[:], ACT.Tanh, scale=0.5)
                act.wait_ge(first_done, k - 3)
                first_gate(k - 3, 2, act_o, 3, 0.5)
                read(u2T[:], psA, u2_done, k - 1, u2T_ready)
                visit(early[2], early[1])
                read_output(k - 2)

            def iteration(s):
                k = s.k
                if s.last:
                    last_iteration(k)
                    return
                if s.mid and not s.prep:
                    exp(s, 0)
                if s.back:
                    read(hn2, hn2, xn2_ready, k - 1, hn2_ready, ACT.Relu)
                if s.front:
                    act.wait_ge(v_done, k + 1)
                    if s.back:
                        act.wait_ge(att_done, 2 * k - 2)
                    a_.activation(v_sb[:, s.par, :, :, 0:HD], psA.rearrange("p (b h d) -> p b h d", b=GB, h=HEADS),
                                  ACT.Copy).then_inc(v_ready, 1)
                    read(qT[:], psQ, q_done, k + 1, q_ready)
                if s.front and not s.back:
                    read(kT[:], psK, k_done, k + 1, k_ready)
                if s.mid and not s.prep:
                    read_probT(s, 0)
                if s.prep and not s.mid:
                    read_weight(2)
                    read_weight(3)
                if s.next1:
                    read_hT(psX[s.back], k + 2, 1 - s.par)
                if s.finish:
                    read_output(k - 3)
                if s.mid and s.prep:
                    exp(s, 0)
                    for m in s.weights:
                        if m == s.weights[3]:
                            read_probT(s, 0)
                        read_weight(m)
                if s.back:
                    read(u1T[:], psA, u1_done, k - 1, u1T_ready)
                if s.mid:
                    exp(s, 1)
                if s.at == GROUPS:
                    a_.activation(sig_i[:, 0, 0:1], bias[:, 0:1], ACT.Sigmoid)
                if s.front and s.back:
                    read(kT[:], psK, k_done, k + 1, k_ready)
                if s.finish:
                    if s.after:
                        act.wait_ge(first_h, k - 3)
                    first_gate(k - 3, 0, act_i, 0, 0.5)
                if s.mid:
                    read_probT(s, 1)
                if s.back:
                    read(h1[:], psA, z1_done, k - 1, h1_ready, ACT.Relu)
                if s.finish:
                    first_gate(k - 3, 1, act_g, 2, 1.0)
                    act.wait_ge(first_cell, k - 2)
                    a_.activation(act_i[:], act_g[:], ACT.Tanh, scale=0.5)
                    if s.after:
                        act.wait_ge(first_done, k - 3)
                    first_gate(k - 3, 2, act_o, 3, 0.5)
                if s.at == GROUPS:
                    act.wait_ge(att_done, 2 * GROUPS)
                    a_.activation(sig_i[:, 0, 0:1], bias[:, 0:1], ACT.Copy).then_inc(gate_acts, 4)
                if s.back:
                    read(u2T[:], psA, u2_done, k - 1, u2T_ready)
                if s.at == GROUPS:
                    visit(early[0], None)

            pipeline(act, iteration)

            walk(act, visit)

            for j in range(1, OUT_GROUPS, 2):
                act.wait_ge(out_ready, j + 1)
                g = GROUPS - OUT_GROUPS + j
                act.dma_start(out[g * GB:(g + 1) * GB, :, :].rearrange("b n d -> n b d"),
                              X[:, g * GB:(g + 1) * GB, :]).then_inc(out_stored, 16)

        @block.tensor
        def _(pe):
            mm = nc.tensor.matmul

            def transposed(to, src, n=GB):
                for b in range(n):
                    last = nc.tensor.transpose(to[:, b * P:(b + 1) * P], src[:, b, :], ident[:])
                return last

            pe.wait_ge(consts, 1)
            pe.wait_ge(w_loaded, 16 * 5)
            nc.tensor.transpose(ps[:, 2, 0:P], adj_sb[:], ident[:])
            nc.tensor.transpose(ps[:, 2, P:P + 2 * C], bias_rows[:], ident[0:2 * C, 0:2 * C]).then_inc(adjT_done, 1)

            def batches(T):
                return T.rearrange("p (b n) -> p b n", b=GB)

            def graph_mix(h, done):
                def part(b):
                    l = mm(psA[:, b * N:(b + 1) * N], h[:, b * D:(b + 1) * D], adjT[:], start=True, stop=True)
                    if b == GB - 1:
                        l.then_inc(done, 1)
                return [lambda b=b: part(b) for b in range(GB)]

            def project(s, psum, column, done):
                wx = slice(column, column + D)

                def part(n):
                    w, h = ((wqk_hi, hT_hi), (wqk_hi, hT_lo), (wqk_lo, hT_hi))[n]
                    l = mm(psum, w[:, wx], h[:, s.par, :], start=n == 0, stop=n == 2)
                    if n == 2:
                        l.then_inc(done, 1)
                return [lambda n=n: part(n) for n in range(3)]

            def graph_linear_1():
                mm(batches(psA), sums_parts[:], bg_parts[:, 0, :].unsqueeze(1).to_broadcast([ROWS, GB, D]),
                   start=True, stop=False)
                for b in range(GB):
                    l = mm(psA[:, b * D:(b + 1) * D], u1T[:, b * N:(b + 1) * N], wg[:, 0, :],
                           start=False, stop=b == GB - 1)
                return l

            def graph_linear_2(s):
                def bias():
                    pe.wait_ge(u2T_ready, s.k - 1)
                    if s.finish:
                        pe.wait_ge(first_acts, s.k * 3 - 6)
                    mm(batches(psB), bg_parts[:, 1, :], sums_parts[:].unsqueeze(1).to_broadcast([ROWS, GB, N]),
                       start=True, stop=False)

                def part(b):
                    at_ = slice(b * N, (b + 1) * N)
                    l = mm(psB[:, at_], wg[:, 1, :], u2T[:, at_], start=False, stop=b == GB - 1)
                    if b == GB - 1:
                        l.then_inc(z2_done, 1)
                return [bias] + [lambda b=b: part(b) for b in range(GB)]

            def first_gate(s, m, gate):
                if not s.finish:
                    return
                g = s.k - 3
                if m == 0:
                    pe.wait_ge(H_ready, g + 1)
                else:
                    pe.wait_ge(first_acts, g * 3 + m)
                wx, at_ = slice(gate * P, (gate + 1) * P), ds(g * GT, GT)
                mm(psB, W_hi[:, 0, 0, wx], H_hi[:, at_], start=True, stop=False)
                mm(psB, W_hi[:, 0, 0, wx], H_lo[:, at_], start=False, stop=False)
                mm(psB, W_lo[:, 0, 0, wx], H_hi[:, at_], start=False, stop=True).then_inc(first_sums, 1)

            def interleave(short, long, first=0):
                for m, one in enumerate(short):
                    one()
                    if m >= first and m - first < len(long):
                        long[m - first]()
                for one in long[max(0, len(short) - first):]:
                    one()

            def transpose_prob(s, half):
                pe.wait_ge(exp_ready, s.k * 2 - 1 + half)
                pv = prob.rearrange("p (h b n) -> p h b n", h=HEADS, b=GB)
                for h in (2 * half, 2 * half + 1):
                    l = transposed(psS[:, h, :], pv[:, h, :, :])
                l.then_inc(probT_done, 1)

            def attend(s, half):
                def part(b):
                    if b == 0:
                        pe.wait_ge(probT_ready, s.k * 2 - 1 + half)
                    for h in (2 * half, 2 * half + 1):
                        o = b * 2 + h % 2
                        l = mm(psO[:, half, o * (HD + 1):(o + 1) * (HD + 1)], probT[:, h, b * N:(b + 1) * N],
                               v_sb[:, 1 - s.par, b, h, :], start=True, stop=True)
                    if b == GB - 1:
                        l.then_inc(att_done, 1)
                return [lambda b=b: part(b) for b in range(GB)]

            def scores(half):
                def part(b):
                    at_ = slice(b * N, (b + 1) * N)
                    for h in (2 * half, 2 * half + 1):
                        rows = slice(h * HD, (h + 1) * HD)
                        l = mm(psS[:, h, at_], qT[rows, at_], kT[rows, at_], start=False, stop=b == GB - 1)
                    if b == GB - 1:
                        l.then_inc(scores_done, 1)
                return [lambda b=b: part(b) for b in range(GB)]

            def put_mask(heads):
                for h in heads:
                    mm(psS[:, h, :].rearrange("p (b n) -> p b n", n=N), ident_bf[:],
                       mask[:].unsqueeze(1).to_broadcast([P, GB, N]), start=True, stop=False)

            def visit(it, prev):
                if it is None:
                    return
                if it.t == OUT:
                    for j in range(OUT_GROUPS):
                        pe.wait_ge(gate_acts, banks_free(it, j))
                        pe.wait_ge(h_sum, it.chunk * OUT_GROUPS + (j + 1))
                        h = finished(it.chunk, j)
                        transposed(ps[:, 4 * it.par + j, :], h.rearrange("p (b n) -> p b n", b=GB))\
                            .then_inc(gate_sums, 1)
                    return
                w = width(it.p)
                if it.p == 1:
                    pe.wait_ge(H_ready, it.chunk + 1)
                if it in early:
                    pe.wait_ge(first_done, (it.chunk + 1) * (BATCHES[2] // BATCHES[1]))
                elif prev is early[-1]:
                    pe.wait_ge(first_done, GROUPS - 1)
                if it.waits:
                    pe.wait_ge(steps, it.needs)
                x_hi, x_lo = tokens(H_hi, it), tokens(H_lo, it)
                for j, gate in enumerate((0, 2, 1, 3)):
                    if it.t == 0 and gate == 1:
                        continue
                    if prev is early[-1] and j == 3:
                        pe.wait_ge(H_ready, GROUPS)
                    pe.wait_ge(gate_acts, banks_free(it, j))
                    to = ps[:, 4 * it.par + j, 0:w]
                    to3 = to.rearrange("k (b w) -> k b w", b=BATCHES[it.p])
                    wx = slice(gate * P, (gate + 1) * P)
                    terms = [(to3, W_hi[:, 0, it.p - 1, wx], x_hi), (to3, W_hi[:, 0, it.p - 1, wx], x_lo),
                             (to3, W_lo[:, 0, it.p - 1, wx], x_hi)]
                    if it.t:
                        s_hi, s_lo = slot(S_hi, it, before=1), slot(S_lo, it, before=1)
                        terms += [(to, W_hi[:, 1, it.p - 1, wx], s_hi), (to, W_hi[:, 1, it.p - 1, wx], s_lo),
                                  (to, W_lo[:, 1, it.p - 1, wx], s_hi)]
                    for m, (o, wt, v) in enumerate(terms):
                        l = mm(o, wt, v, start=m == 0, stop=m == len(terms) - 1)
                    l.then_inc(gate_sums, 2 if it.t == 0 and j == 1 else 1)

            pe.wait_ge(xn_ready, 1)
            transposed(psB, xn).then_inc(xnT_done, 1)

            pe.wait_ge(ones_set, 1)
            pe.wait_ge(prep_done, 1)
            mm(ps[0:ROWS, 3, 0:N], ones_f[:], adjT[:], start=True, stop=True).then_inc(sums_done, 1)

            def transpose_weight(m):
                w = wst[m // MAX_SKIP][:, GATES * (m % MAX_SKIP):GATES * (m % MAX_SKIP + 1), :]
                transposed(psW(m), w).then_inc(wT_done, 1)

            pe.wait_ge(wih_loaded, 16)
            transpose_weight(0)
            transpose_weight(1)

            def last_iteration(s):
                k = s.k
                visit(early[1], early[0])
                pe.wait_ge(hn2_ready, k - 1)
                interleave([], graph_mix(hn2, u1_done))
                first_gate(s, 0, 0)
                pe.wait_ge(u1T_ready, k - 1)
                graph_linear_1().then_inc(z1_done, 1)
                first_gate(s, 1, 2)
                pe.wait_ge(h1_ready, k - 1)
                interleave([], graph_mix(h1, u2_done))
                first_gate(s, 2, 3)
                visit(early[2], early[1])
                interleave([], graph_linear_2(s))

            def iteration(s):
                k = s.k
                if s.last:
                    last_iteration(s)
                    return
                if s.front:
                    pe.wait_ge(hT_ready, k + 1)
                    if s.at == 2:
                        pe.wait_ge(w_lo_done, 2 * MAX_SKIP)
                    if s.finish:
                        pe.wait_ge(u2T_ready, k - 2)
                    for b in range(GB):
                        l = mm(psA[:, b * D:(b + 1) * D], hT[:, b * N:(b + 1) * N], wv[:], start=True, stop=True)
                    l.then_inc(v_done, 1)
                    pe.wait_ge(hT_lo_ready, k + 1)
                    if s.back:
                        pe.wait_ge(att_read, 2 * k - 2)
                    if not s.mid:
                        pe.wait_ge(wqk_ready, 1)
                    interleave([], project(s, psQ, 0, q_done))
                    if s.prep:
                        interleave([], project(s, psK, D, k_done))
                    if not s.mid:
                        transpose_weight(2)
                        pe.wait_ge(sums_ready, 1)
                        transpose_weight(3)
                if s.mid and not s.prep:
                    transpose_prob(s, 0)
                if s.next1:
                    pe.wait_ge(xn_ready, k + 2)
                    transposed(psX[s.back], xn).then_inc(xnT_done, 1)
                if s.mid and s.prep:
                    pe.wait_ge(whh_loaded, 16)
                    pe.wait_ge(q_ready, k + 1)
                    pe.wait_ge(v_ready, k + 1)
                    for m in s.weights:
                        if m == s.weights[2]:
                            pe.wait_ge(hT_hi_ready, k + 2)
                        if m == s.weights[3]:
                            transpose_prob(s, 0)
                            pe.wait_ge(w_lo_done, m - 2)
                        transpose_weight(m)
                if s.back:
                    pe.wait_ge(hn2_ready, k - 1)
                    if s.front:
                        pe.wait_ge(v_ready, k + 1)
                    for part in graph_mix(hn2, u1_done):
                        part()
                keys = project(s, psK, D, k_done) if s.front and s.back else []
                if keys and s.next1:
                    keys[0] = lambda first=keys[0]: (pe.wait_ge(hT_hi_ready, k + 2), first())
                if s.mid:
                    if s.front:
                        pe.wait_ge(q_ready, k + 1)
                    if s.prep:
                        pe.wait_ge(w_lo_done, 2 * MAX_SKIP - 2)
                    interleave(attend(s, 0), keys, first=1)
                first_gate(s, 0, 0)
                if s.mid:
                    transpose_prob(s, 1)
                if s.back:
                    pe.wait_ge(u1T_ready, k - 1)
                    if s.at == 2:
                        pe.wait_ge(wg_loaded, 32)
                        pe.wait_ge(bg_ready, 1)
                    graph_linear_1().then_inc(z1_done, 1)
                first_gate(s, 1, 2)
                masks = []
                if s.front:
                    if not s.mid:
                        pe.wait_ge(w_lo_done, 2)
                    put_mask((0, 1))
                    if s.mid:
                        pe.wait_ge(probT_ready, k * 2)
                        pe.wait_ge(k_ready, k + 1)
                    masks = [lambda h=h: put_mask((h,)) for h in (2, 3)]
                if s.mid:
                    interleave(attend(s, 1), masks)
                first_gate(s, 2, 3)
                mix, linear = [], []
                if s.back:
                    pe.wait_ge(h1_ready, k - 1)
                    mix, linear = graph_mix(h1, u2_done), graph_linear_2(s)
                if s.front:
                    pe.wait_ge(k_ready, k + 1)
                interleave(scores(0) if s.front else [], mix)
                if s.at == GROUPS:
                    visit(early[0], None)
                if not s.mid:
                    pe.wait_ge(w_lo_done, MAX_SKIP)
                    put_mask((2, 3))
                interleave(scores(1) if s.front else [], linear, first=1)

            pipeline(pe, iteration)

            walk(pe, visit)

        @block.vector
        def _(dve):
            v_ = nc.vector

            def moments(layer, g, stats_ready, var):
                for b in range(GB):
                    l = v_.bn_stats(stats[:, layer, b, :], X[:, ds(g * GB + b, 1), :].rearrange("p a d -> p (a d)"))
                l.then_inc(stats_ready, 1)
                dve.wait_ge(stats_ready, g + 1)
                v_.memset(pause[:], 0.0)
                for b in range(GB):
                    l = v_.bn_aggr(mv[:, layer, b, :], stats[:, layer, b, :])
                l.then_inc(var, 1)

            def normalize(layer, g, to, rstd_ready, ready):
                dve.wait_ge(rstd_ready, g + 1)
                for b in range(GB):
                    l = v_.tensor_scalar(to[:, b, :], X[:, ds(g * GB + b, 1), :].rearrange("p a d -> p (a d)"),
                                         mv[:, layer, b, 0:1], rstd[:, layer, b:b + 1], ALU.subtract, ALU.mult)
                l.then_inc(ready, 1)

            def split_hT(count, par):
                dve.wait_ge(hT_hi_ready, count)
                v_.tensor_tensor(hT_lo[:, par, :], hT, hT_hi[:, par, :].bitcast(F32), ALU.subtract)\
                    .then_inc(hT_lo_ready, 1)

            def split_weight(m):
                dve.wait_ge(w_hi_done, m + 1)
                v_.tensor_tensor(W_lo[:, m // MAX_SKIP, m % MAX_SKIP, :], psW(m),
                                 W_hi[:, m // MAX_SKIP, m % MAX_SKIP, :].bitcast(F32), ALU.subtract)\
                    .then_inc(w_lo_done, 1)

            v_.memset(ones_f[:], 1.0).then_inc(ones_set, 1)
            dve.wait_ge(x_loaded, 16)
            moments(0, 0, stats1, var1)
            normalize(0, 0, xn, rstd1, xn_ready)
            dve.wait_ge(adjT_done, 1)
            v_.tensor_scalar(mask[:], adj_sb[:], 0.0, MASKED, ALU.is_equal, ALU.mult)
            v_.tensor_copy(adjT[:], ps[:, 2, 0:P])
            v_.tensor_copy(bias_2[:], ps[:, 2, P:P + 2 * C]).then_inc(prep_done, 1)
            dve.wait_ge(wqk_hi_ready, 1)
            v_.tensor_tensor(wqk_lo[:], wqk_raw, wqk_hi[:].bitcast(F32), ALU.subtract).then_inc(wqk_ready, 1)
            dve.wait_ge(x_loaded, 32)
            moments(0, 1, stats1, var1)
            split_hT(1, 0)
            dve.wait_ge(sums_done, 1)
            v_.tensor_copy(sums_parts[:], ps[0:ROWS, 3, 0:N]).then_inc(sums_hi, 1)
            dve.wait_ge(sums_hi, 1)
            mid, end = slice(PART, 2 * PART), slice(2 * PART, ROWS)
            v_.tensor_tensor(sums_parts[mid, :], ps[mid, 3, 0:N], sums_parts[mid, :].bitcast(F32), ALU.subtract)\
                .then_inc(sums_ready, 1)
            split_weight(0)
            split_weight(1)
            dve.wait_ge(xnT_done, 1)
            normalize(0, 1, xn, rstd1, xn_ready)
            split_weight(2)
            split_weight(3)
            v_.tensor_tensor(bias[:], bias_2[:, 0:C], bias_2[:, C:2 * C], ALU.add).then_inc(bias_ready, 1)
            dve.wait_ge(bias_ready, 1)
            v_.tensor_scalar(half_bias[:], bias[:, 0:GATES], 0.5, None, ALU.mult)
            dve.wait_ge(bg_loaded, 16 * 6)
            v_.tensor_copy(bg_parts[:], bg_rows[:]).then_inc(parts_hi, 1)
            dve.wait_ge(parts_hi, 1)
            v_.tensor_tensor(bg_parts[end, :, :], bg_rows[end, :, :], bg_parts[end, :, :].bitcast(F32), ALU.subtract)\
                .then_inc(bg_ready, 1)

            s3 = psS.rearrange("p h (b n) -> p (h b) n", n=N)
            o4 = psO[:, :, 0:2 * GB * (HD + 1)].rearrange("p a (b h d) -> p a b h d", h=2, d=HD + 1)
            rec4 = rec[:].rearrange("p (a b h) -> p a b h", a=2, h=2)
            att5 = att.rearrange("p (b a h d) -> p a b h d", a=2, h=2, d=HD)

            def shift(s, half):
                dve.wait_ge(scores_done, s.k * 2 - 1 + half)
                part = slice(2 * half * GB, 2 * (half + 1) * GB)
                v_.tensor_reduce(rmax[:, part], s3[:, part, :], AX_X, ALU.max).then_inc(max_ready, 1)
                dve.wait_ge(max_ready, s.k * 2 - 1 + half)
                v_.tensor_tensor(prob.rearrange("p (c n) -> p c n", n=N)[:, part, :], s3[:, part, :],
                                 rmax[:, part].unsqueeze(2).to_broadcast([P, 2 * GB, N]), ALU.subtract)\
                    .then_inc(shifted, 1)

            def over_sums(s, half):
                dve.wait_ge(att_done, s.k * 2 - 1 + half)
                v_.reciprocal(rec4[:, half], o4[:, half, :, :, HD]).then_inc(rec_ready, 1)
                dve.wait_ge(rec_ready, s.k * 2 - 1 + half)
                v_.tensor_tensor(att5[:, half], o4[:, half, :, :, 0:HD],
                                 rec4[:, half].unsqueeze(3).to_broadcast([P, GB, 2, HD]), ALU.mult).then_inc(att_read, 1)
                dve.wait_ge(att_read, s.k * 2 - 1 + half)
                heads = slice(half * 2 * HD, (half + 1) * 2 * HD)
                xg = X[:, ds(s.k * GB - GB, GB), heads]
                v_.tensor_tensor(xg, xg, att.rearrange("p (b d) -> p b d", b=GB)[:, :, heads], ALU.add)\
                    .then_inc(x2_ready, 1)

            def first_cell_part(g):
                dve.wait_ge(first_acts, g * 3 + 2)
                v_.scalar_tensor_tensor(act_g[:], act_i[:], 1.0, act_g[:], ALU.add, ALU.mult).then_inc(first_cell, 1)

            def first_h_part(g):
                dve.wait_ge(first_acts, g * 3 + 3)
                v_.scalar_tensor_tensor(act_o[:], act_o[:], 1.0, act_i[:], ALU.add, ALU.mult).then_inc(first_h, 1)

            def first_split(g):
                at_ = ds(g * GT, GT)
                dve.wait_ge(first_h, g + 1)
                v_.tensor_scalar(H_hi[:, at_], act_o[:], 0.5, None, ALU.mult).then_inc(first_hi, 1)
                dve.wait_ge(first_hi, g + 1)
                v_.scalar_tensor_tensor(H_lo[:, at_], act_o[:], 0.5, H_hi[:, at_].bitcast(F32),
                                        ALU.mult, ALU.subtract).then_inc(first_done, 1)

            def output_lo(g):
                dve.wait_ge(H_hi_ready, g + 1)
                at_ = ds(g * GT, GT)
                v_.scalar_tensor_tensor(H_lo[:, at_], psB, 0.0, H_hi[:, at_].bitcast(F32),
                                        ALU.max, ALU.subtract).then_inc(H_ready, 1)

            def cell_part(it):
                w = width(it.p)
                c = slot(cell, it)
                dve.wait_ge(gate_acts, gates_read(it, 2 if it.t == 0 else 3))
                if it.t == 0:
                    v_.tensor_tensor(c, sig_i[:, it.buf, 0:w], tanh_g[:, it.buf, 0:w], ALU.mult).then_inc(cells, 1)
                    return
                v_.tensor_tensor(c, sig_f[:, it.buf, 0:w], slot(cell, it, before=1), ALU.mult).then_inc(fc_ready, 1)
                dve.wait_ge(fc_ready, it.later + 1)
                dve.wait_ge(ig_ready, it.later + 1)
                v_.tensor_tensor(c, c, ig[:, it.buf, 0:w], ALU.add).then_inc(cells, 1)

            def state(it):
                w = width(it.p)
                dve.wait_ge(gate_acts, gates_read(it, 4))
                dve.wait_ge(tanhs, it.steps + 1)
                v_.tensor_tensor(h_f[:, it.buf, 0:w], sig_o[:, it.buf, 0:w], tanh_c[:, it.buf, 0:w], ALU.mult)\
                    .then_inc(h_f_ready, 1)

            def split(it):
                h = h_f[:, it.buf, 0:width(it.p)]
                if it.t == it.p - 1:
                    hi, lo = tokens(H_hi, it), tokens(H_lo, it)
                    h = h.rearrange("k (b w) -> k b w", b=BATCHES[it.p])
                else:
                    hi, lo = slot(S_hi, it), slot(S_lo, it)
                dve.wait_ge(h_f_ready, it.steps + (2 + 1))
                v_.tensor_scalar(hi, h, 1.0, None, ALU.mult).then_inc(s_hi_ready, 1)
                dve.wait_ge(s_hi_ready, it.steps + 1)
                v_.tensor_tensor(lo, h, hi.bitcast(F32), ALU.subtract).then_inc(steps, 1)

            def add_parts(chunk, j):
                at_ = slice((chunk * OUT_GROUPS + j) * GT, (chunk * OUT_GROUPS + j + 1) * GT)
                return v_.tensor_tensor(finished(chunk, j), H_hi[:, at_].bitcast(F32), H_lo[:, at_].bitcast(F32),
                                        ALU.add)

            def last_state(it):
                dve.wait_ge(gate_acts, gates_read(it, 4))
                dve.wait_ge(tanhs, it.steps + 1)
                dve.wait_ge(most_ready, OUT_GROUPS)
                p, w = it.p, GT // it.p
                first = cell[:, 0:(OUT_GROUPS - 1) * GT]
                for to, at_, groups in ((first, slice(0, (OUT_GROUPS - 1) * w), OUT_GROUPS - 1),
                                        (spare, slice((OUT_GROUPS - 1) * w, OUT_GROUPS * w), 1)):
                    v_.tensor_tensor(to.rearrange("k (w q) -> k w q", q=p)[:, :, p - 1], sig_o[:, it.buf, at_],
                                     tanh_c[:, it.buf, at_], ALU.mult).then_inc(h_sum, groups)

            def whole(it):
                dve.wait_ge(steps, it.steps + 1)
                for j in range(OUT_GROUPS):
                    if it.chunk == CHUNKS[MAX_SKIP] - 2:
                        add_parts(it.chunk + 1, j).then_inc(most_ready, 1)
                    if it.chunk:
                        dve.wait_ge(x_added, (it.chunk - 1) * OUT_GROUPS + j + 1)
                    add_parts(it.chunk, j).then_inc(h_sum, 1)

            def visit(it, prev):
                if prev and prev.t != OUT and is_last(prev):
                    last_state(prev)
                    return
                if prev and prev.t != OUT:
                    state(prev)
                    if not (it and it.t == 0):
                        split(prev)
                if it and it.t != OUT:
                    cell_part(it)
                if prev and prev.t != OUT:
                    if it and it.t == 0:
                        split(prev)
                    if prev.p == MAX_SKIP and prev.t == prev.p - 1:
                        whole(prev)
                if it and it.t == OUT and it.chunk == CHUNKS[MAX_SKIP] - 1:
                    for j in range(OUT_GROUPS):
                        g = it.chunk * OUT_GROUPS + j
                        dve.wait_ge(gate_sums, it.n * 4 + (j + 1))
                        xg = X[:, g * GB:(g + 1) * GB, :]
                        v_.tensor_tensor(xg, xg, ps[:, 4 * it.par + j, :].rearrange("p (b d) -> p b d", b=GB), ALU.add)\
                            .then_inc(out_ready, 1)

            def last_iteration(k):
                v_.memset(released[:, 0:1], 0.0).then_inc(cells, 2)
                v_.memset(released[:, 1:2], 0.0).then_inc(h_f_ready, 2)
                normalize(1, k - 2, xn2, rstd2, xn2_ready)
                output_lo(k - 3)
                visit(early[0], None)
                first_h_part(k - 4)
                first_split(k - 4)
                visit(early[1], early[0])
                first_cell_part(k - 3)
                first_h_part(k - 3)
                first_split(k - 3)
                visit(early[2], early[1])
                output_lo(k - 2)

            def iteration(s):
                k = s.k
                if s.last:
                    last_iteration(k)
                    return
                if s.mid:
                    shift(s, 0)
                if s.back:
                    normalize(1, k - 2, xn2, rstd2, xn2_ready)
                if s.mid:
                    shift(s, 1)
                if s.prep and s.mid:
                    for m in s.weights:
                        split_weight(m)
                if s.next2:
                    dve.wait_ge(x_loaded, k * 16 + 48)
                    moments(0, k + 2, stats1, var1)
                if s.finish:
                    output_lo(k - 3)
                if s.after:
                    first_h_part(k - 4)
                if s.next2:
                    dve.wait_ge(xnT_done, k + 2)
                    normalize(0, k + 2, xn, rstd1, xn_ready)
                if s.mid:
                    over_sums(s, 0)
                if s.after:
                    first_split(k - 4)
                if s.next1:
                    split_hT(k + 2, 1 - s.par)
                if s.finish:
                    first_cell_part(k - 3)
                if s.mid:
                    over_sums(s, 1)
                    dve.wait_ge(x2_ready, 2 * k)
                    moments(1, k - 1, stats2, var2)

            pipeline(dve, iteration)

            walk(dve, visit)


_INS = ['x', 'adj', 'L0_gnn_W', 'L1_gnn_Wg0', 'L1_gnn_bg0', 'L1_gnn_Wg1', 'L1_gnn_bg1', 'L1_gnn_Wih', 'L1_gnn_Whh',
        'L1_gnn_bih', 'L1_gnn_bhh']


def kernel(**inputs):
    import numpy as _np
    import concourse.bacc as _bacc
    from concourse import mybir as _mybir
    from concourse.bass_utils import run_bass_kernel_spmd as _run

    nc = _bacc.Bacc("TRN2", target_bir_lowering=False, num_devices=1)
    arrays, args = {}, []
    for name in _INS:
        a = _np.ascontiguousarray(inputs[name])
        arrays[f"in_{name}_dram"] = a
        args.append(nc.dram_tensor(f"in_{name}_dram", a.shape, _mybir.dt.from_np(a.dtype), kind="ExternalInput").ap())
    shape = inputs['x'].shape
    args.append(nc.dram_tensor("out_0_dram", shape, _mybir.dt.float32, kind="ExternalOutput").ap())
    gnn_block(nc, *args)
    r = _run(nc, [arrays], core_ids=[0])
    return r.results[0]["out_0_dram"]
```
